# Optimizing a Trainium2 kernel written in Bass

```python
import numpy as np
import jax
import jax.numpy as jnp

def _softmax(x, axis=-1):
    return jax.nn.softmax(x, axis=axis)

def _gelu(x):
    return jax.nn.gelu(x, approximate=True)

def _silu(x):
    return jax.nn.silu(x)

def _sigmoid(x):
    return jax.nn.sigmoid(x)

def _layernorm(x, axis=-1, eps=1e-05):
    m = jnp.mean(x, axis=axis, keepdims=True)
    v = jnp.var(x, axis=axis, keepdims=True)
    return (x - m) / jnp.sqrt(v + eps)

def _scatter_add(tgt, idx, src, axis=0):
    return tgt.at[idx].add(src)

def _segment_sum(src, seg, n):
    return jax.ops.segment_sum(src, seg, n)
kernel_name = 'mk_adj_ffn_d1_adj_r2_2e9622'

def setup_inputs(seed: int=0):
    np.random.seed(seed)
    _w = jnp.asarray

    def _rec_inputs():
        import jax
        import jax.numpy as jnp
        _gk = jax.random.key(seed)
        x = -0.0005207 + 1.001 * jax.random.normal(jax.random.fold_in(_gk, 1), (64, 128, 128), jnp.float32)
        _w = (1.0 + jnp.arange(128, dtype=jnp.float32)) ** (-0.5)
        _w = _w / _w.mean()
        _pij = jnp.clip(0.0625 * _w[:, None] * _w[None, :], 0.0, 1.0)
        _a = jax.random.uniform(jax.random.fold_in(_gk, 2), (64, 128, 128)) < _pij
        adj = _a.astype(jnp.int32)
        return (x, adj)
    x, adj = _rec_inputs()

    def _L0_gnn_setup():
        import jax, jax.numpy as jnp
        import numpy as np
        ALPHA = 0.2
        NEG_INF = -9000000000000000.0
        key = jax.random.key(seed)
        k_h, k_adj, k_W, k_a = jax.random.split(key, 4)
        B, N, Din, Dout = (8, 512, 128, 128)
        h = jax.random.normal(k_h, (B, N, Din), dtype=jnp.float32)
        adj = jax.random.randint(k_adj, (B, N, N), 0, 2, dtype=jnp.int32)
        W = jax.random.normal(k_W, (Dout, Din), dtype=jnp.float32) * (1.0 / np.sqrt(Din))
        lim = np.float32(1.414 * np.sqrt(6.0 / (2 * Dout + 1)))
        a = jax.random.uniform(k_a, (2 * Dout, 1), dtype=jnp.float32, minval=-lim, maxval=lim)
        return {'h': h, 'adj': adj, 'W': W, 'a': a}
    _L0_gnn_all = _L0_gnn_setup()
    _L0_gnn_in = {k: v for k, v in _L0_gnn_all.items() if k in ('W', 'a')}
    del _L0_gnn_all

    def _L0_ffn_setup():
        import jax, jax.numpy as jnp
        import numpy as np
        D_MODEL = 128
        N_EXPERTS = 16
        HIDDEN = 256
        SCALE = 0.02
        key = jax.random.key(seed)
        ks = jax.random.split(key, 5)
        x = jax.random.normal(ks[0], (4, 4096, D_MODEL), dtype=jnp.float32)
        gate_w = jax.random.normal(ks[1], (D_MODEL, N_EXPERTS), dtype=jnp.float32) * SCALE
        gate_b = jnp.zeros((N_EXPERTS,), dtype=jnp.float32)
        w1 = jax.random.normal(ks[2], (N_EXPERTS, D_MODEL, HIDDEN), dtype=jnp.float32) * SCALE
        w2 = jax.random.normal(ks[3], (N_EXPERTS, D_MODEL, HIDDEN), dtype=jnp.float32) * SCALE
        w3 = jax.random.normal(ks[4], (N_EXPERTS, HIDDEN, D_MODEL), dtype=jnp.float32) * SCALE
        return {'x': x, 'gate_w': gate_w, 'gate_b': gate_b, 'w1': w1, 'w2': w2, 'w3': w3}
    _L0_ffn_all = _L0_ffn_setup()
    _L0_ffn_in = {k: v for k, v in _L0_ffn_all.items() if k in ('gate_w', 'gate_b', 'w1', 'w2', 'w3')}
    del _L0_ffn_all
    return {'x': x, 'adj': adj, 'L0_gnn_W': _L0_gnn_in['W'], 'L0_gnn_a': _L0_gnn_in['a'], 'L0_ffn_gate_w': _L0_ffn_in['gate_w'], 'L0_ffn_gate_b': _L0_ffn_in['gate_b'], 'L0_ffn_w1': _L0_ffn_in['w1'], 'L0_ffn_w2': _L0_ffn_in['w2'], 'L0_ffn_w3': _L0_ffn_in['w3']}

def reference(x, adj, L0_gnn_W, L0_gnn_a, L0_ffn_gate_w, L0_ffn_gate_b, L0_ffn_w1, L0_ffn_w2, L0_ffn_w3):
    import jax
    import jax.numpy as jnp

    def _L0_gnn_ref(h, adj, W, a):
        import jax, jax.numpy as jnp
        import numpy as np
        ALPHA = 0.2
        NEG_INF = -9000000000000000.0
        Wh = jnp.einsum('bnd,fd->bnf', h, W)
        F_ = Wh.shape[-1]
        a1 = a[:F_, 0]
        a2 = a[F_:, 0]
        src = Wh @ a1
        dst = Wh @ a2
        e = src[:, :, None] + dst[:, None, :]
        e = jnp.where(e > 0, e, ALPHA * e)
        e = jnp.where(adj > 0, e, NEG_INF)
        attention = jax.nn.softmax(e, axis=-1)
        h_prime = jnp.einsum('bij,bjf->bif', attention, Wh)
        return h_prime

    def _L0_ffn_ref(x, gate_w, gate_b, w1, w2, w3):
        import jax, jax.numpy as jnp
        import numpy as np
        D_MODEL = 128
        N_EXPERTS = 16
        HIDDEN = 256
        SCALE = 0.02
        n_experts = w1.shape[0]
        logits = jnp.einsum('bsd,de->bse', x, gate_w) + gate_b
        probs = jax.nn.softmax(logits, axis=-1)
        top_probs, top_idx = jax.lax.top_k(probs, 2)
        top_probs = top_probs / jnp.sum(top_probs, axis=-1, keepdims=True)
        dispatch = jnp.sum(jax.nn.one_hot(top_idx, n_experts, dtype=x.dtype) * top_probs[..., None], axis=-2)
        h1 = jnp.einsum('bsd,edh->bseh', x, w1)
        h2 = jnp.einsum('bsd,edh->bseh', x, w2)
        hidden = jax.nn.silu(h1) * h2
        expert_out = jnp.einsum('bseh,eho->bseo', hidden, w3)
        return jnp.einsum('bseo,bse->bso', expert_out, dispatch)
    x = x + _L0_gnn_ref(_layernorm(x, axis=-1), adj, L0_gnn_W, L0_gnn_a)
    x = x + _L0_ffn_ref(_layernorm(x, axis=-1), L0_ffn_gate_w, L0_ffn_gate_b, L0_ffn_w1, L0_ffn_w2, L0_ffn_w3)
    return x

_drawn_inputs = setup_inputs


def setup_inputs(seed=0):
    import zlib

    import numpy as np

    out = dict(_drawn_inputs(seed))
    spreads = {'L0_ffn_gate_b': (0.0, 0.8)}
    factors = {'L0_ffn_gate_w': 8.0, 'L0_ffn_w1': 8.0, 'L0_ffn_w2': 8.0, 'L0_ffn_w3': 8.0}
    for name, (base, spread) in spreads.items():
        noise = np.random.default_rng([zlib.crc32(name.encode()), seed]).standard_normal(out[name].shape)
        drawn = base * np.exp(spread * noise) if base else spread * noise
        out[name] = jnp.asarray(drawn.astype(out[name].dtype))
    for name, factor in factors.items():
        out[name] = (out[name] * factor).astype(out[name].dtype)
    return out
```

```python
import concourse.bass as bass
from concourse import mybir
from contextlib import ExitStack

F32 = mybir.dt.float32
BF16 = mybir.dt.bfloat16
I32 = mybir.dt.int32
U32 = mybir.dt.uint32
ALU = mybir.AluOpType
ACT = mybir.ActivationFunctionType
AX = mybir.AxisListType


def gat_moe_kernel(nc: bass.Bass, x, adj, gnn_w, gnn_a, gate_w, gate_b, w1, w2, w3, out):
    NG, N, D = x.shape
    P = 128
    assert N == P and D == P
    GG = 4
    NI = NG // GG
    NE = gate_w.shape[1]
    HID = w1.shape[2]
    HC = HID // P
    SLOPE, EPS = 0.2, 1e-5
    MASKED = 9e15 / SLOPE
    NSEG = 2
    TS = NG // NSEG
    IS = NI // NSEG
    QT = 4
    NT = -(-(2 * TS + NE - 1) // QT) * QT
    QS = NT // QT
    NQ = NSEG * QS
    ZC = NT // IS
    assert ZC * IS == NT

    xs = [nc.dram_tensor(f"sorted_rows{s}", (NT * P, D), F32, kind="Internal").ap() for s in range(NSEG)]
    ys = [nc.dram_tensor(f"expert_rows{s}", (NT * P, D), F32, kind="Internal").ap() for s in range(NSEG)]

    ctx = ExitStack()
    with ctx:
        def sb(name, shape, dt=F32):
            return ctx.enter_context(nc.sbuf_tensor(name, shape, dt))

        def sem(name):
            return ctx.enter_context(nc.semaphore(name))

        X = sb("X", [P, NG, D])
        H2 = sb("H2", [P, NG, D])
        W12 = sb("W12", [P, NE * 2 * HID])
        W3 = sb("W3", [P, NE * HC * D])
        LG = sb("LG", [P, NG, NE])
        GATE = sb("GATE", [P, 2, NG])
        ROW = sb("ROW", [P, NSEG, 2, TS], U32)
        EID = sb("EID", [1, NSEG * NT], I32)
        ident = sb("ident", [P, P])
        before = sb("before", [P, P])
        before_bf = sb("before_bf", [P, P], BF16)
        ones_bf = sb("ones_bf", [P, P], BF16)
        e_before = sb("e_before", [P, NE, NE])
        e_rank = sb("e_rank", [P, NE])
        tile_rows = sb("tile_rows", [P, TS])
        tile_no = sb("tile_no", [1, NT])
        half_neg = sb("half_neg", [P, 2 * GG])
        zeros = sb("zeros", [P, ZC * D])
        Wg = sb("Wg", [P, D])
        a12 = sb("a12", [P, 2])
        a12b = sb("a12b", [P, 2, P])
        WgT = sb("WgT", [P, P])
        src_w = sb("src_w", [P, P])
        dst_w = sb("dst_w", [P, P])
        gw = sb("gw", [P, NE])
        gb = sb("gb", [P, NE])
        adj_t = sb("adj_t", [P, 2, GG * N], I32)
        stats = sb("stats", [P, 2, 2 * GG, 6])
        mv = sb("mv", [P, 2, 2 * GG, 2])
        var_eps = sb("var_eps", [P, 2, 2 * GG])
        rstd = sb("rstd", [P, 2, 2 * GG])
        h = sb("h", [P, 2, GG * D])
        hT = sb("hT", [P, 2, GG * N])
        Wh = sb("Wh", [P, 2, GG * D])
        mask = sb("mask", [P, 2, GG * N])
        em = sb("em", [P, GG * N])
        lr = sb("lr", [P, 2, GG * N])
        neg_max = sb("neg_max", [P, 2, GG])
        row_sum = sb("row_sum", [P, 2, GG])
        row_inv = sb("row_inv", [P, GG])
        prob = sb("prob", [P, 2, GG * N])
        probT = sb("probT", [P, GG * N])
        h2 = sb("h2", [P, 2, GG * D])
        h2T = sb("h2T", [P, GG * N])
        TE = TS * NE
        r_m = sb("r_m", [P, 4, TS])
        r_a = sb("r_a", [P, TE])
        r_b = sb("r_b", [P, TE])
        r_l2 = sb("r_l2", [P, TE])
        oh = sb("oh", [P, 2, TE])
        r_e = sb("r_e", [P, 3, TS])
        chosen = sb("chosen", [P, TE], BF16)
        cnt = sb("cnt", [TS, NE], BF16)
        cnt_b = sb("cnt_b", [TS, TE], BF16)
        r_c = sb("r_c", [P, NE, TS])
        r_ee = sb("r_ee", [P, NE, NE])
        r_t = sb("r_t", [P, 4, NE])
        r_row = sb("r_row", [P, 2, TS])
        r_idf = sb("r_idf", [1, NT])
        r_id = sb("r_id", [1, NT, NE - 1])
        xs_t = sb("xs_t", [P, 2, QT, D])
        xT = sb("xT", [P, 2, QT * P])
        sil = sb("sil", [P, 2, HID])
        hid = sb("hid", [P, 2, HID])
        hidT = sb("hidT", [P, 2, HID])
        yo = sb("yo", [P, 2, QT * D])
        got = hT[:].rearrange("p a (b k d) -> p (a b) k d", b=2, d=D)
        part = h[:, 0, :].rearrange("p (a d) -> p a d", d=D)
        res = h[:, 1, :].rearrange("p (a d) -> p a d", d=D)

        bank = [ctx.enter_context(nc.psum_tensor(f"bank{i}", [P, 512], F32)) for i in range(8)]

        loaded = [sem(f"loaded{i}") for i in range(2)]
        small_in = sem("small_in")
        weights_in = sem("weights_in")
        zeroed = [sem(f"zeroed{s}") for s in range(NSEG)]
        consts = sem("consts")
        const_steps = sem("const_steps")
        setup_v = sem("setup_v")
        setup_p = sem("setup_p")
        bn1, bn2, ag1, ag2 = sem("bn1"), sem("bn2"), sem("ag1"), sem("ag2")
        var_ready, rstd_ready = sem("var_ready"), sem("rstd_ready")
        h_ready, h_turned, hT_ready = sem("h_ready"), sem("h_turned"), sem("hT_ready")
        e_done, wh_done, wh_ready = sem("e_done"), sem("wh_done"), sem("wh_ready")
        mask_ready, em_ready, lr_ready = sem("mask_ready"), sem("em_ready"), sem("lr_ready")
        max_ready, exp_done = sem("max_ready"), sem("exp_done")
        prob_turned, probT_ready, att_done = sem("prob_turned"), sem("probT_ready"), sem("att_done")
        inv_ready, x2_ready = sem("inv_ready"), sem("x2_ready")
        h2_kept = [sem(f"h2_kept{i}") for i in range(2)]
        h2_ready, h2_turned, h2T_ready = sem("h2_ready"), sem("h2_turned"), sem("h2T_ready")
        logits_done, logits_ready = sem("logits_done"), sem("logits_ready")
        r_steps, r_diff, r_exp = sem("r_steps"), sem("r_diff"), sem("r_exp")
        r_chosen, r_counted, r_cnt, r_pos = sem("r_chosen"), sem("r_counted"), sem("r_cnt"), sem("r_pos")
        rows_ready, eid_ready = sem("rows_ready"), sem("eid_ready")
        scattered = [sem(f"scattered{s}") for s in range(NSEG)]
        xs_in, xs_turned, xT_ready = sem("xs_in"), sem("xs_turned"), sem("xT_ready")
        up_done, silu_ready, hid_ready = sem("up_done"), sem("silu_ready"), sem("hid_ready")
        hid_turned, hidT_ready, down_done = sem("hid_turned"), sem("hidT_ready"), sem("down_done")
        yo_ready, y_stored = sem("yo_ready"), sem("y_stored")
        gathered = [sem(f"gathered{i}") for i in range(4)]
        part_ready, res_ready = sem("part_ready"), sem("res_ready")
        out_stored = [sem(f"out_stored{i}") for i in range(2)]

        block = ctx.enter_context(nc.Block())

        C0 = NQ - 1 - 2 * (TS // 4)

        def later(n, least):
            return not isinstance(n, int) or n >= least

        def phases(eng, iteration, route):
            def peeled(i):
                steps = {-1: i + 1 < NI, 0: i < NI, 1: 1 <= i <= NI, 2: i >= 2}
                iteration(i, i % 2, lambda k: steps[k])

            for i in range(4):
                peeled(i)
            with eng.Fori(0, (IS + 2 - 4) // 2) as r:
                i = r * 2 + 4
                iteration(i, 0)
                iteration(i + 1, 1)
            route(0)
            with eng.Fori(0, (NI - 2 - (IS + 2)) // 2) as r:
                i = r * 2 + (IS + 2)
                iteration(i, 0)
                iteration(i + 1, 1)
            for i in range(NI - 2, NI + 2):
                peeled(i)
            route(1)

        x_v = x.rearrange("g n d -> n g d")
        adj_v = adj.rearrange("g n m -> n g m")
        out_v = out.rearrange("g n d -> n g d")

        @block.sync
        def _(sp):
            def load_group(i, par):
                if later(i, 2):
                    sp.wait_ge(mask_ready, i - 1)
                sp.dma_start(X[:, bass.ds(i * GG, GG), :], x_v[:, bass.ds(i * GG, GG), :]).then_inc(loaded[par], 16)
                sp.dma_start(adj_t[:, par, :].rearrange("p (g m) -> p g m", g=GG),
                             adj_v[:, bass.ds(i * GG, GG), :]).then_inc(loaded[par], 16)

            def zero_rows(s, c):
                sp.dma_start(xs[s][bass.ds(c * ZC * P, ZC * P), :].rearrange("(t p) n -> p t n", p=P),
                             zeros[:].rearrange("p (t n) -> p t n", n=D)).then_inc(zeroed[s], 16)

            def keep(k, par):
                sp.wait_ge(h2_ready, k + 1)
                sp.dma_start(H2[:, bass.ds(k * GG, GG), :],
                             h2[:, par, :].rearrange("p (g d) -> p g d", d=D)).then_inc(h2_kept[par], 16)

            load_group(0, 0)
            sp.dma_start(Wg[:], gnn_w).then_inc(small_in, 16)
            for k in range(2):
                sp.dma_start(a12[:, k:k + 1], gnn_a[k * D:(k + 1) * D, :]).then_inc(small_in, 16)
            sp.dma_start(gw[:], gate_w).then_inc(small_in, 16)
            sp.dma_start(gb[:], gate_b.rearrange("(o e) -> o e", o=1).broadcast_to([P, NE])).then_inc(small_in, 16)
            load_group(1, 1)
            sp.wait_ge(consts, 1)
            for c in range(4):
                load_group(c + 2, c % 2)
                if c >= 2:
                    keep(c - 2, c % 2)
                zero_rows(0, c)
            with sp.Fori(0, (IS - 4) // 2) as r:
                c = r * 2 + 4
                for odd in range(2):
                    load_group(c + odd + 2, odd)
                    keep(c + odd - 2, odd)
                    zero_rows(0, c + odd)
            w12 = W12[:].rearrange("p (e k h) -> p e k h", e=NE, k=2)
            sp.dma_start(w12[:, :, 0, :], w1.rearrange("e d h -> d e h")).then_inc(weights_in, 16)
            sp.dma_start(w12[:, :, 1, :], w2.rearrange("e d h -> d e h")).then_inc(weights_in, 16)
            sp.dma_start(W3[:].rearrange("p (e c o) -> p e c o", e=NE, c=HC),
                         w3.rearrange("e (c p) o -> p e c o", p=P)).then_inc(weights_in, 16)
            with sp.Fori(0, (NI - 2 - IS) // 2) as r:
                c = r * 2 
                for odd in range(2):
                    load_group(c + odd + IS + 2, odd)
                    keep(c + odd + IS - 2, odd)
                    zero_rows(1, c + odd)
            for c in range(NI - 2 - IS, IS):
                zero_rows(1, c)
            for k in range(NI - 4, NI):
                keep(k, k % 2)

            def load_quad(s, n, par):
                if later(n, 2):
                    sp.wait_ge(xs_turned, n - 1)
                if later(n, 1):
                    sp.wait_ge(xs_in, 16 * n)
                sp.dma_start(xs_t[:, par, :, :],
                             xs[s][bass.ds((n - s * QS) * QT * P, QT * P), :].rearrange("(t p) n -> p t n", p=P))\
                  .then_inc(xs_in, 16)

            def store_half(t, half):
                sp.wait_ge(res_ready, t + 2)
                sp.dma_start(out_v[:, bass.ds(t, 2), :], res[:, 2 * half:2 * half + 2, :]).then_inc(out_stored[half], 16)

            sp.wait_ge(scattered[0], 16 * 2 * TS)
            load_quad(0, 0, 0)
            load_quad(0, 1, 1)
            with sp.Fori(0, (QS - 1 - 1) // 2) as r:
                q = r * 2 + 1
                load_quad(0, q + 1, 0)
                load_quad(0, q + 2, 1)
            sp.wait_ge(scattered[1], 16 * 2 * TS)
            with sp.Fori(0, (C0 - (QS - 1)) // 2) as r:
                q = r * 2 + (QS - 1)
                load_quad(1, q + 1, 0)
                load_quad(1, q + 2, 1)
            with sp.Fori(0, (NQ - 1 - C0) // 2) as r:
                q = r * 2 + C0
                load_quad(1, q + 1, 0)
                load_quad(1, q + 2, 1)
                store_half(r * 4, 0)
                store_half(r * 4 + 2, 1)
            with sp.Fori(0, (NG - TS) // 4) as r:
                t = r * 4 + TS
                store_half(t, 0)
                store_half(t + 2, 1)
            for half in range(2):
                sp.wait_ge(out_stored[half], 16 * NG // 4)

        @block.tensor
        def _(pe):
            TH, TP, TH2, E, WH, HP, LO, RT = bank
            pe.wait_ge(small_in, 80)
            pe.wait_ge(const_steps, 9)
            pe.wait_ge(setup_v, 1)
            nc.tensor.transpose(TH[:, 0:P], Wg[:], ident[:])
            nc.tensor.matmul(TH[:, P:2 * P], Wg[:], a12b[:, 0, :], start=True, stop=True)
            nc.tensor.matmul(TH[:, 2 * P:3 * P], Wg[:], a12b[:, 1, :], start=True, stop=True).then_inc(setup_p, 1)
            pe.wait_ge(setup_v, 4)

            def turn(dst, src, last):
                for g in range(GG):
                    ins = nc.tensor.transpose(dst[:, g * P:(g + 1) * P], src(g), ident[:])
                ins.then_inc(last, 1)

            def iteration(i, par, has=lambda k: True):
                if has(0):
                    pe.wait_ge(h_ready, i + 1)
                    if later(i, 1):
                        pe.wait_ge(hT_ready, i)
                    turn(TH, lambda g: h[:, par, g * D:(g + 1) * D], h_turned)
                if has(1):
                    j = i - 1
                    if later(j, 1):
                        pe.wait_ge(probT_ready, j)
                    for g in range(GG):
                        pe.wait_ge(exp_done, j * GG + g + 1)
                        ins = nc.tensor.transpose(TP[:, g * P:(g + 1) * P], prob[:, 1 - par, g * N:(g + 1) * N], ident[:])
                    ins.then_inc(prob_turned, 1)
                    pe.wait_ge(probT_ready, j + 1)
                    pe.wait_ge(wh_ready, j + 1)
                    if later(j, 1):
                        pe.wait_ge(x2_ready, j)
                    for g in range(GG):
                        ins = nc.tensor.matmul(HP[:, g * D:(g + 1) * D], probT[:, g * N:(g + 1) * N],
                                               Wh[:, 1 - par, g * D:(g + 1) * D], start=True, stop=True)
                    ins.then_inc(att_done, 1)
                if has(0):
                    pe.wait_ge(hT_ready, i + 1)
                    if later(i, 1):
                        pe.wait_ge(em_ready, i)
                    nc.tensor.matmul(E[:], dst_w[:], hT[:, par, :], start=True, stop=False)
                    for g in range(GG):
                        ins = nc.tensor.matmul(E[:, g * N:(g + 1) * N], hT[:, par, g * N:(g + 1) * N], src_w[:],
                                               start=False, stop=(g == GG - 1))
                    ins.then_inc(e_done, 1)
                    if later(i, 1):
                        pe.wait_ge(wh_ready, i)
                    for g in range(GG):
                        ins = nc.tensor.matmul(WH[:, g * D:(g + 1) * D], hT[:, par, g * N:(g + 1) * N], WgT[:],
                                               start=True, stop=True)
                    ins.then_inc(wh_done, 1)
                if has(2):
                    k = i - 2
                    pe.wait_ge(h2_ready, k + 1)
                    if later(k, 1):
                        pe.wait_ge(h2T_ready, k)
                    turn(TH2, lambda g: h2[:, par, g * D:(g + 1) * D], h2_turned)
                    pe.wait_ge(h2T_ready, k + 1)
                    if later(k, 1):
                        pe.wait_ge(logits_ready, k)
                    for g in range(GG):
                        ins = nc.tensor.matmul(LO[:, g * NE:(g + 1) * NE], h2T[:, g * N:(g + 1) * N], gw[:],
                                               start=True, stop=True)
                    ins.then_inc(logits_done, 1)

            def route(s):
                pe.wait_ge(r_chosen, s + 1)
                tab = chosen[:].rearrange("p (t e) -> p t e", e=NE)
                for e in range(NE):
                    ins = nc.tensor.matmul(LO[0:TS, 64 + e:65 + e], tab[:, :, e], ones_bf[:, 0:1], start=True, stop=True)
                ins.then_inc(r_counted, 1)
                pe.wait_ge(r_cnt, 2 * s + 1)
                nc.tensor.matmul(LO[:, 128:128 + NE], ones_bf[0:TS, :], cnt[:], start=True, stop=True)
                pe.wait_ge(r_cnt, 2 * s + 2)
                nc.tensor.matmul(RT[:, 0:TE], before_bf[:], chosen[:], start=True, stop=False)
                nc.tensor.matmul(RT[:, 0:TE], ones_bf[0:TS, :], cnt_b[:], start=False, stop=True).then_inc(r_pos, 1)

            phases(pe, iteration, route)

            XP, H0, H1, T0, T1, O0, O1, _ = bank
            H, HT, O = (H0, H1), (T0, T1), (O0, O1)
            pe.wait_ge(weights_in, 48)
            pe.wait_ge(eid_ready, NSEG)
            pe.wait_ge(rows_ready, NSEG)

            def expert(t):
                return pe.value_load(EID[0:1, bass.ds(t, 1)], min_val=0, max_val=NE - 1)

            def turn_rows(q, par):
                pe.wait_ge(xs_in, 16 * (q + 1))
                if later(q, 1):
                    pe.wait_ge(xT_ready, q)
                turn(XP, lambda k: xs_t[:, par, k, :], xs_turned)

            def up(t, k, q, par, e):
                if k == 0:
                    pe.wait_ge(xT_ready, q + 1)
                if later(t, 2):
                    pe.wait_ge(hid_ready, t - 1)
                nc.tensor.matmul(H[k % 2][:, 0:2 * HID], xT[:, par, k * P:(k + 1) * P],
                                 W12[:, bass.ds(e * (2 * HID), 2 * HID)], start=True, stop=True).then_inc(up_done, 1)

            def down(t, k, q, par, e):
                pe.wait_ge(hidT_ready, t + 1)
                if k == 0 and later(q, 2):
                    pe.wait_ge(yo_ready, q - 1)
                for c in range(HC):
                    ins = nc.tensor.matmul(O[par][:, k * D:(k + 1) * D], hidT[:, k % 2, c * P:(c + 1) * P],
                                           W3[:, bass.ds(e * (HC * D) + c * D, D)], start=(c == 0), stop=(c == HC - 1))
                ins.then_inc(down_done, 1)

            def quad(q, par, first=False, last=False):
                e = None if first else expert(q * QT - 1)
                e_now = expert(q * QT)
                for k in range(QT):
                    t = q * QT + k
                    if not (last and k == QT - 1):
                        e_next = expert(t + 1)
                        if k < QT - 1:
                            up(t + 1, k + 1, q, par, e_next)
                        else:
                            up(t + 1, 0, q + 1, 1 - par, e_next)
                    if k == 1 and not last:
                        turn_rows(q + 1, 1 - par)
                    if not (first and k == 0):
                        if k == 0:
                            down(t - 1, QT - 1, q - 1, 1 - par, e)
                        else:
                            down(t - 1, k - 1, q, par, e)
                    pe.wait_ge(hid_ready, t + 1)
                    if later(t, 2):
                        pe.wait_ge(hidT_ready, t - 1)
                    for c in range(HC):
                        ins = nc.tensor.transpose(HT[k % 2][:, c * P:(c + 1) * P], hid[:, k % 2, c * P:(c + 1) * P], ident[:])
                    ins.then_inc(hid_turned, 1)
                    e, e_now = e_now, e_next
                if last:
                    down(t, QT - 1, q, par, e)

            turn_rows(0, 0)
            up(0, 0, 0, 0, expert(0))
            quad(0, 0, first=True)
            quad(1, 1)
            quad(2, 0)
            with pe.Fori(0, (NQ - 1 - 3) // 2) as r:
                q = r * 2 + 3
                quad(q, 1)
                quad(q + 1, 0)
            quad(NQ - 1, 1, last=True)

        @block.scalar
        def _(act):
            TH, TP, TH2, E, WH, HP, LO, RT = bank

            def iteration(i, par, has=lambda k: True):
                if has(0):
                    act.wait_ge(loaded[par], 32 * (i // 2) + 32 if isinstance(i, int) else (i - par) * 16 + 32)
                    if later(i, 2):
                        act.wait_ge(em_ready, i - 1)
                    nc.scalar.activation(mask[:, par, :], adj_t[:, par, :], ACT.Relu, scale=2 * MASKED).then_inc(mask_ready, 1)
                    act.wait_ge(h_turned, i + 1)
                    if later(i, 2):
                        act.wait_ge(wh_done, i - 1)
                    nc.scalar.activation(hT[:, par, :], TH[:], ACT.Copy).then_inc(hT_ready, 1)
                if has(1):
                    j = i - 1
                    act.wait_ge(prob_turned, j + 1)
                    if later(j, 1):
                        act.wait_ge(att_done, j)
                    nc.scalar.activation(probT[:], TP[:], ACT.Copy).then_inc(probT_ready, 1)
                if has(0):
                    act.wait_ge(wh_done, i + 1)
                    if later(i, 2):
                        act.wait_ge(att_done, i - 1)
                    nc.scalar.activation(Wh[:, par, :], WH[:], ACT.Copy).then_inc(wh_ready, 1)
                if has(2):
                    k = i - 2
                    act.wait_ge(h2_turned, k + 1)
                    if later(k, 1):
                        act.wait_ge(logits_done, k)
                    nc.scalar.activation(h2T[:], TH2[:], ACT.Copy).then_inc(h2T_ready, 1)
                if has(0):
                    act.wait_ge(max_ready, i + 1)
                    if later(i, 2):
                        act.wait_ge(prob_turned, i - 1)
                        act.wait_ge(inv_ready, i - 1)
                    for g in range(GG):
                        nc.scalar.activation(prob[:, par, g * N:(g + 1) * N], lr[:, par, g * N:(g + 1) * N], ACT.Exp,
                                             bias=neg_max[:, par, g:g + 1],
                                             accum_out=row_sum[:, par, g:g + 1]).then_inc(exp_done, 1)

            def route(s):
                act.wait_ge(r_diff, s + 1)
                nc.scalar.activation(r_e[:, 1, :], r_e[:, 0, :], ACT.Exp).then_inc(r_exp, 1)

            phases(act, iteration, route)

            XP, H0, H1, T0, T1, O0, O1, _ = bank
            H, O = (H0, H1), (O0, O1)

            def copy_rows(q, par):
                act.wait_ge(xs_turned, q + 1)
                if later(q, 2):
                    act.wait_ge(up_done, (q - 1) * QT)
                nc.scalar.activation(xT[:, par, :], XP[:], ACT.Copy).then_inc(xT_ready, 1)

            def silu(t, k):
                act.wait_ge(up_done, t + 1)
                if later(t, 2):
                    act.wait_ge(hid_ready, t - 1)
                nc.scalar.activation(sil[:, k % 2, :], H[k % 2][:, 0:HID], ACT.Silu).then_inc(silu_ready, 1)

            def copy_out(q, par):
                act.wait_ge(down_done, (q + 1) * QT)
                if later(q, 2):
                    act.wait_ge(y_stored, 16 * (q - 1))
                nc.scalar.activation(yo[:, par, :], O[par][:], ACT.Copy).then_inc(yo_ready, 1)

            def store_out(s, q, par):
                act.wait_ge(yo_ready, q + 1)
                if later(q, 1):
                    act.wait_ge(y_stored, 16 * q)
                act.dma_start(ys[s][bass.ds((q - s * QS) * QT * P, QT * P), :].rearrange("(t p) n -> p t n", p=P),
                              yo[:, par, :].rearrange("p (t n) -> p t n", n=D)).then_inc(y_stored, 16)

            def quad(q, par, s_prev, first=False, last=False):
                for k in range(QT):
                    if not (last and k == QT - 1):
                        silu(q * QT + k + 1, k + 1)
                    if k == 1 and not last:
                        copy_rows(q + 1, 1 - par)
                    if k == 2 and not first:
                        copy_out(q - 1, 1 - par)
                    if k == 3 and not first:
                        store_out(s_prev, q - 1, 1 - par)

            copy_rows(0, 0)
            silu(0, 0)
            quad(0, 0, 0, first=True)
            quad(1, 1, 0)
            quad(2, 0, 0)
            with act.Fori(0, (QS + 1 - 3) // 2) as r:
                q = r * 2 + 3
                quad(q, 1, 0)
                quad(q + 1, 0, 0)
            with act.Fori(0, (NQ - 1 - (QS + 1)) // 2) as r:
                q = r * 2 + (QS + 1)
                quad(q, 1, 1)
                quad(q + 1, 0, 1)
            quad(NQ - 1, 1, 1, last=True)
            copy_out(NQ - 1, 1)
            store_out(1, NQ - 1, 1)

        @block.vector
        def _(dve):
            TH, TP, TH2, E, WH, HP, LO, RT = bank
            V = nc.vector
            dve.wait_ge(small_in, 80)
            for k in range(2):
                ins = V.tensor_copy(a12b[:, k, :], a12[:, k:k + 1].broadcast_to([P, P]))
            ins.then_inc(setup_v, 1)
            dve.wait_ge(setup_p, 1)
            V.tensor_copy(WgT[:], TH[:, 0:P]).then_inc(setup_v, 1)
            V.tensor_copy(src_w[:], TH[:, P:2 * P]).then_inc(setup_v, 1)
            V.tensor_copy(dst_w[:], TH[:, 2 * P:3 * P]).then_inc(setup_v, 1)

            def carry():
                dve.wait_ge(const_steps, 10)

            def row(t, i, g):
                return t[:, bass.ds(i * GG + g, 1), :].rearrange("p a d -> p (a d)")

            def stats_of(i, batch_par, col, bn):
                for g in range(GG):
                    ins = V.bn_stats(stats[:, batch_par, col + g, :], row(X, i, g))
                ins.then_inc(bn, 1)

            def aggregate(batch_par, col, ag):
                for g in range(GG):
                    V.bn_aggr(mv[:, batch_par, col + g, :], stats[:, batch_par, col + g, :]).then_inc(ag, 1)

            def normalize(i, dst, col, batch_par):
                for g in range(GG):
                    ins = V.tensor_scalar(dst(g), row(X, i, g), mv[:, batch_par, col + g, 0:1],
                                          rstd[:, batch_par, col + g:col + g + 1], ALU.subtract, ALU.mult)
                return ins

            def first_stats(i, par):
                dve.wait_ge(loaded[par], 32 * (i // 2) + 32 if isinstance(i, int) else (i - par) * 16 + 32)
                return i

            def iteration(i, par, has=lambda k: True):
                if has(0) or has(2):
                    dve.wait_ge(rstd_ready, i + 1)
                if has(0):
                    if later(i, 2):
                        dve.wait_ge(h_turned, i - 1)
                    normalize(i, lambda g: h[:, par, g * D:(g + 1) * D], 0, 1 - par).then_inc(h_ready, 1)
                if has(2):
                    k = i - 2
                    if later(k, 2):
                        dve.wait_ge(h2_turned, k - 1)
                        dve.wait_ge(h2_kept[par], k // 2 * 16 if isinstance(k, int) else (k - par) * 8)
                    normalize(k, lambda g: h2[:, par, g * D:(g + 1) * D], GG, 1 - par).then_inc(h2_ready, 1)
                if has(-1):
                    carry()
                    first_stats(i + 1, 1 - par)
                    stats_of(i + 1, par, 0, bn1)
                    dve.wait_ge(bn1, i + 2)
                if has(1):
                    j = i - 1
                    dve.wait_ge(exp_done, (j + 1) * GG)
                    V.reciprocal(row_inv[:], row_sum[:, 1 - par, :]).then_inc(inv_ready, 1)
                if has(-1):
                    aggregate(par, 0, ag1)
                if has(1):
                    dve.wait_ge(inv_ready, j + 1)
                    dve.wait_ge(att_done, j + 1)
                    for g in range(GG):
                        ins = V.scalar_tensor_tensor(row(X, j, g), HP[:, g * D:(g + 1) * D], row_inv[:, g:g + 1],
                                                     row(X, j, g), ALU.mult, ALU.add)
                    ins.then_inc(x2_ready, 1)
                    carry()
                    dve.wait_ge(x2_ready, j + 1)
                    stats_of(j, par, GG, bn2)
                    dve.wait_ge(bn2, j + 1)
                if has(0):
                    dve.wait_ge(e_done, i + 1)
                    dve.wait_ge(mask_ready, i + 1)
                    if later(i, 1):
                        dve.wait_ge(lr_ready, i)
                    V.scalar_tensor_tensor(em[:], mask[:, par, :], -MASKED, E[:], ALU.add, ALU.min).then_inc(em_ready, 1)
                if has(1):
                    aggregate(par, GG, ag2)
                lo, hi = (0 if has(-1) else GG), (2 * GG if has(1) else GG)
                if hi > lo:
                    if has(-1):
                        dve.wait_ge(ag1, (i + 2) * GG)
                    if has(1):
                        dve.wait_ge(ag2, i * GG)
                    V.tensor_scalar(var_eps[:, par, lo:hi], mv[:, par, lo:hi, 1], EPS, None, ALU.add).then_inc(var_ready, 1)
                if has(0):
                    dve.wait_ge(em_ready, i + 1)
                    if later(i, 2):
                        dve.wait_ge(exp_done, (i - 1) * GG)
                    V.scalar_tensor_tensor(lr[:, par, :], em[:], SLOPE, em[:], ALU.mult, ALU.max).then_inc(lr_ready, 1)
                if has(2):
                    k = i - 2
                    dve.wait_ge(logits_done, k + 1)
                    V.tensor_tensor(LG[:, bass.ds(k * GG, GG), :], LO[:, 0:GG * NE].rearrange("p (g e) -> p g e", e=NE),
                                    gb[:].rearrange("p (o e) -> p o e", o=1).broadcast_to([P, GG, NE]), ALU.add)\
                        .then_inc(logits_ready, 1)
                if has(0):
                    dve.wait_ge(lr_ready, i + 1)
                    V.tensor_reduce(neg_max[:, par, :], lr[:, par, :].rearrange("p (g m) -> p g m", m=N), AX.X, ALU.max,
                                    negate=True).then_inc(max_ready, 1)

            steps = [0]

            def link(ins):
                steps[0] += 1
                ins.then_inc(r_steps, 1)
                dve.wait_ge(r_steps, steps[0])

            def te(ap):
                return ap.rearrange("p (t e) -> p t e", e=NE)

            def route(s):
                def per_tile(ap):
                    return ap.rearrange("p (t o) -> p t o", o=1).broadcast_to([P, TS, NE])

                def per_expert(ap, n):
                    return ap.rearrange("p (o e) -> p o e", o=1).broadcast_to([P, n, NE])

                dve.wait_ge(logits_ready, (s + 1) * IS)
                logits = LG[:, s * TS:(s + 1) * TS, :]
                for c in range(2):
                    L = logits if c == 0 else te(r_l2[:])
                    link(V.tensor_reduce(r_m[:, c, :], L, AX.X, ALU.max))
                    link(V.tensor_tensor(te(r_a[:]), L, per_tile(r_m[:, c, :]), ALU.is_equal))
                    link(V.tensor_tensor(te(r_b[:]), te(r_a[:]), per_expert(e_rank[:], TS), ALU.mult))
                    link(V.tensor_reduce(r_m[:, 2 + c, :], te(r_b[:]), AX.X, ALU.max))
                    link(V.tensor_tensor(te(oh[:, c, :]), te(r_b[:]), per_tile(r_m[:, 2 + c, :]), ALU.is_equal))
                    if c == 0:
                        link(V.scalar_tensor_tensor(r_l2[:], oh[:, 0, :], -3e38,
                                                    logits.rearrange("p t e -> p (t e)"), ALU.mult, ALU.add))
                V.tensor_tensor(chosen[:], oh[:, 0, :], oh[:, 1, :], ALU.add).then_inc(r_chosen, 1)
                V.tensor_tensor(r_e[:, 0, :], r_m[:, 1, :], r_m[:, 0, :], ALU.subtract).then_inc(r_diff, 1)
                dve.wait_ge(r_counted, s + 1)
                V.tensor_copy(cnt[:], LO[0:TS, 64:64 + NE]).then_inc(r_cnt, 1)
                dve.wait_ge(r_cnt, 2 * s + 1)
                V.tensor_tensor(te(cnt_b[:]),
                                before[0:TS, 0:TS].rearrange("p (t o) -> p t o", o=1).broadcast_to([TS, TS, NE]),
                                cnt[:].rearrange("p (o e) -> p o e", o=1).broadcast_to([TS, TS, NE]), ALU.mult).then_inc(r_cnt, 1)
                gates = GATE[:, :, s * TS:(s + 1) * TS]
                dve.wait_ge(r_exp, s + 1)
                link(V.tensor_scalar(r_e[:, 2, :], r_e[:, 1, :], 1.0, None, ALU.add))
                link(V.reciprocal(gates[:, 0, :], r_e[:, 2, :]))
                link(V.tensor_tensor(gates[:, 1, :], r_e[:, 1, :], gates[:, 0, :], ALU.mult))
                dve.wait_ge(r_pos, s + 1)
                total = LO[:, 128:128 + NE]
                link(V.tensor_tensor(r_c[:], total.rearrange("p (e o) -> p e o", o=1).broadcast_to([P, NE, TS]),
                                     tile_rows[:].rearrange("p (o j) -> p o j", o=1).broadcast_to([P, NE, TS]), ALU.is_gt))
                link(V.tensor_reduce(r_t[:, 0, :], r_c[:], AX.X, ALU.add))
                link(V.tensor_tensor(r_ee[:], e_before[:], per_expert(r_t[:, 0, :], NE), ALU.mult))
                link(V.tensor_reduce(r_t[:, 1, :], r_ee[:], AX.X, ALU.add))
                link(V.tensor_scalar(r_t[:, 3, :], r_t[:, 1, :], float(P), None, ALU.mult))
                link(V.tensor_tensor(te(r_a[:]), te(RT[:, 0:TE]), per_expert(r_t[:, 3, :], TS), ALU.add))
                for c in range(2):
                    link(V.tensor_tensor(r_b[:], oh[:, c, :], r_a[:], ALU.mult))
                    link(V.tensor_reduce(r_row[:, c, :], te(r_b[:]), AX.X, ALU.add))
                link(V.tensor_tensor(r_t[:, 2, :], r_t[:, 1, :], r_t[:, 0, :], ALU.add))
                V.tensor_copy(ROW[:, s, :, :], r_row[:]).then_inc(rows_ready, 1)
                dve.wait_ge(rows_ready, s + 1)
                link(V.tensor_tensor(r_id[:], r_t[0:1, 2, 0:NE - 1].rearrange("p (o e) -> p o e", o=1).broadcast_to([1, NT, NE - 1]),
                                     tile_no[:].rearrange("p (j o) -> p j o", o=1).broadcast_to([1, NT, NE - 1]), ALU.is_le))
                link(V.tensor_reduce(r_idf[:], r_id[:], AX.X, ALU.add))
                V.tensor_copy(EID[0:1, s * NT:(s + 1) * NT], r_idf[:]).then_inc(eid_ready, 1)

            dve.wait_ge(const_steps, 10)
            first_stats(0, 0)
            stats_of(0, 1, 0, bn1)
            dve.wait_ge(bn1, 1)
            aggregate(1, 0, ag1)
            dve.wait_ge(ag1, GG)
            V.tensor_scalar(var_eps[:, 1, 0:GG], mv[:, 1, 0:GG, 1], EPS, None, ALU.add).then_inc(var_ready, 1)
            phases(dve, iteration, route)

            XP, H0, H1, T0, T1, O0, O1, _ = bank
            H, HT = (H0, H1), (T0, T1)

            def gate_hidden(t, k):
                dve.wait_ge(silu_ready, t + 1)
                if later(t, 2):
                    dve.wait_ge(hid_turned, t - 1)
                V.tensor_tensor(hid[:, k % 2, :], sil[:, k % 2, :], H[k % 2][:, HID:2 * HID], ALU.mult).then_inc(hid_ready, 1)

            def quad(q, last=False):
                for k in range(QT):
                    t = q * QT + k
                    dve.wait_ge(hid_turned, t + 1)
                    if later(t, 2):
                        dve.wait_ge(down_done, t - 1)
                    V.tensor_copy(hidT[:, k % 2, :], HT[k % 2][:, 0:HID]).then_inc(hidT_ready, 1)
                    if not (last and k == QT - 1):
                        gate_hidden(t + 1, k + 1)

            def combine(t, slot, first):
                dve.wait_ge(gathered[slot], t * 8 + (32 - 8 * slot))
                def weight(c):
                    return GATE[:, c, bass.ds(t, 1)]
                V.scalar_tensor_tensor(part[:, slot, :], got[:, slot, 0, :], weight(0),
                                       X[:, bass.ds(t, 1), :].rearrange("p a d -> p (a d)"), ALU.mult, ALU.add)\
                    .then_inc(part_ready, 1)
                if not first:
                    dve.wait_ge(out_stored[slot // 2], t * 4 - 4 * slot)
                dve.wait_ge(part_ready, t + 1)
                V.scalar_tensor_tensor(res[:, slot, :], got[:, slot, 1, :], weight(1), part[:, slot, :],
                                       ALU.mult, ALU.add).then_inc(res_ready, 1)

            gate_hidden(0, 0)
            for q in range(3):
                quad(q)
            with dve.Fori(0, (C0 - 3) // 2) as r:
                q = r * 2 + 3
                quad(q)
                quad(q + 1)

            def with_combine(q, t, first):
                quad(q)
                combine(t, 0, first)
                combine(t + 1, 1, first)
                quad(q + 1)
                combine(t + 2, 2, first)
                combine(t + 3, 3, first)
            with_combine(C0, 0, True)
            with dve.Fori(0, (NQ - 1 - (C0 + 2)) // 2) as r:
                q = r * 2 + (C0 + 2)
                with_combine(q, r * 4 + 4, False)
            quad(NQ - 1, last=True)
            with dve.Fori(0, (NG - TS) // 4) as r:
                t = r * 4 + TS
                for slot in range(4):
                    combine(t + slot, slot, False)

        @block.gpsimd
        def _(pool):
            g = nc.gpsimd
            g.memset(zeros[:], 0.0).then_inc(consts, 1)
            g.memset(half_neg[:], -0.5).then_inc(const_steps, 1)
            g.memset(ident[:], 0.0).then_inc(const_steps, 1)
            g.memset(before[:], 1.0).then_inc(const_steps, 1)
            g.memset(ones_bf[:], 1.0).then_inc(const_steps, 1)
            g.memset(e_before[:], 1.0).then_inc(const_steps, 1)
            pool.wait_ge(const_steps, 5)
            g.affine_select(out=ident[:], in_=ident[:], compare_op=ALU.not_equal, fill=1.0, base=0,
                            pattern=[[-1, P]], channel_multiplier=1).then_inc(const_steps, 1)
            g.affine_select(out=before[:], in_=before[:], compare_op=ALU.is_gt, fill=0.0, base=0,
                            pattern=[[1, P]], channel_multiplier=-1).then_inc(const_steps, 1)
            g.affine_select(out=e_before[:], in_=e_before[:], compare_op=ALU.is_gt, fill=0.0, base=0,
                            pattern=[[1, NE], [-1, NE]], channel_multiplier=0).then_inc(const_steps, 1)
            pool.wait_ge(const_steps, 8)
            g.tensor_copy(before_bf[:], before[:]).then_inc(const_steps, 1)
            g.iota(e_rank[:], pattern=[[-1, NE]], base=NE, channel_multiplier=0, allow_small_or_imprecise_dtypes=True)
            g.iota(tile_rows[:], pattern=[[P, TS]], base=0, channel_multiplier=0, allow_small_or_imprecise_dtypes=True)
            g.iota(tile_no[:], pattern=[[1, NT]], base=0, channel_multiplier=0, allow_small_or_imprecise_dtypes=True).then_inc(const_steps, 1)

            def root(i):
                par = i % 2
                lo, hi = (0 if i + 1 < NI else GG), (2 * GG if i >= 1 else GG)
                pool.wait_ge(var_ready, i + 2)
                if i >= 1:
                    pool.wait_ge(h_ready, min(i, NI))
                if i >= 3:
                    pool.wait_ge(h2_ready, i - 2)
                g.tensor_tensor(rstd[:, par, lo:hi], var_eps[:, par, lo:hi], half_neg[:, lo:hi], ALU.pow).then_inc(rstd_ready, 1)

            def scatter(s, n):
                t, c = n // 2, n % 2
                pool.indirect_dma_start(xs[s], bass.IndirectOffsetOnAxis(ap=ROW[:, s, c, t:t + 1], axis=0),
                                        H2[:, s * TS + t, :], None).then_inc(scattered[s], 16)

            n = 0
            for i in range(-1, NI + 1):
                root(i)
                if i == IS + 1:
                    pool.wait_ge(zeroed[0], 16 * IS)
                    pool.wait_ge(rows_ready, 1)
                    for par in range(2):
                        pool.wait_ge(h2_kept[par], 8 * IS)
                if i > IS:
                    for _ in range(6):
                        scatter(0, n)
                        n += 1
            for m in range(n, 2 * TS):
                scatter(0, m)
            pool.wait_ge(zeroed[1], 16 * IS)
            pool.wait_ge(rows_ready, 2)
            for par in range(2):
                pool.wait_ge(h2_kept[par], 8 * NI)
            for m in range(2 * TS):
                scatter(1, m)
            for s in range(NSEG):
                pool.wait_ge(y_stored, 16 * QS * (s + 1))
                for t in range(TS):
                    n = s * TS + t
                    if n >= 4:
                        pool.wait_ge(res_ready, n - 3)
                    for c in range(2):
                        pool.indirect_dma_start(got[:, n % 4, c, :], None, ys[s],
                                                bass.IndirectOffsetOnAxis(ap=ROW[:, s, c, t:t + 1], axis=0))\
                            .then_inc(gathered[n % 4], 16)


_INS = ['x', 'adj', 'L0_gnn_W', 'L0_gnn_a', 'L0_ffn_gate_w', 'L0_ffn_gate_b', 'L0_ffn_w1', 'L0_ffn_w2', 'L0_ffn_w3']
_OUTS = [((64, 128, 128), 'float32')]


def kernel(**inputs):
    import numpy as _np
    import concourse.bacc as _bacc
    from concourse import mybir as _mybir
    from concourse.bass_utils import run_bass_kernel_spmd as _run

    nc = _bacc.Bacc("TRN2", target_bir_lowering=False, num_devices=1)
    arrays, args = {}, []
    for name in _INS:
        a = _np.ascontiguousarray(inputs[name])
        arrays[f"in_{name}_dram"] = a
        args.append(nc.dram_tensor(f"in_{name}_dram", a.shape, _mybir.dt.from_np(a.dtype), kind="ExternalInput").ap())
    for i, (shape, dtype) in enumerate(_OUTS):
        dt = _mybir.dt.from_np(_np.dtype(dtype))
        args.append(nc.dram_tensor(f"out_{i}_dram", shape, dt, kind="ExternalOutput").ap())
    gat_moe_kernel(nc, *args)
    r = _run(nc, [arrays], core_ids=[0])
    return r.results[0]["out_0_dram"]
```

```python
import concourse.bass as bass
from concourse import mybir
from contextlib import ExitStack

F32 = mybir.dt.float32
BF16 = mybir.dt.bfloat16
I32 = mybir.dt.int32
U32 = mybir.dt.uint32
ALU = mybir.AluOpType
ACT = mybir.ActivationFunctionType
AX = mybir.AxisListType


def gat_moe_kernel(nc: bass.Bass, x, adj, gnn_w, gnn_a, gate_w, gate_b, w1, w2, w3, out):
    NG, N, D = x.shape
    P = 128
    assert N == P and D == P
    GG = 4
    NI = NG // GG
    NE = gate_w.shape[1]
    HID = w1.shape[2]
    HC = HID // P
    SLOPE, EPS = 0.2, 1e-5
    MASKED = 9e15 / SLOPE
    NSEG = 2
    TS = NG // NSEG
    IS = NI // NSEG
    QT = 4
    NT = -(-(2 * TS + NE - 1) // QT) * QT
    QS = NT // QT
    NQ = NSEG * QS
    ZC = NT // IS
    assert ZC * IS == NT

    xs = [nc.dram_tensor(f"sorted_rows{s}", (NT * P, D), F32, kind="Internal").ap() for s in range(NSEG)]
    ys = [nc.dram_tensor(f"expert_rows{s}", (NT * P, D), F32, kind="Internal").ap() for s in range(NSEG)]

    ctx = ExitStack()
    with ctx:
        def sb(name, shape, dt=F32):
            return ctx.enter_context(nc.sbuf_tensor(name, shape, dt))

        def sem(name):
            return ctx.enter_context(nc.semaphore(name))

        X = sb("X", [P, NG, D])
        H2 = sb("H2", [P, NG, D])
        W12 = sb("W12", [P, NE * 2 * HID])
        W3 = sb("W3", [P, NE * HC * D])
        LG = sb("LG", [P, NG, NE])
        GATE = sb("GATE", [P, 2, NG])
        ROW = sb("ROW", [P, NSEG, 2, TS], U32)
        EID = sb("EID", [1, NSEG * NT], I32)
        ident = sb("ident", [P, P])
        before = sb("before", [P, P])
        before_bf = sb("before_bf", [P, P], BF16)
        ones_bf = sb("ones_bf", [P, P], BF16)
        e_before = sb("e_before", [P, NE, NE])
        e_rank = sb("e_rank", [P, NE])
        tile_rows = sb("tile_rows", [P, TS])
        tile_no = sb("tile_no", [1, NT])
        half_neg = sb("half_neg", [P, 2 * GG])
        zeros = sb("zeros", [P, ZC * D])
        Wg = sb("Wg", [P, D])
        a12 = sb("a12", [P, 2])
        a12b = sb("a12b", [P, 2, P])
        WgT = sb("WgT", [P, P])
        src_w = sb("src_w", [P, P])
        dst_w = sb("dst_w", [P, P])
        gw = sb("gw", [P, NE])
        gb = sb("gb", [P, NE])
        adj_t = sb("adj_t", [P, 2, GG * N], I32)
        stats = sb("stats", [P, 2, 2 * GG, 6])
        mv = sb("mv", [P, 2, 2 * GG, 2])
        var_eps = sb("var_eps", [P, 2, 2 * GG])
        rstd = sb("rstd", [P, 2, 2 * GG])
        h = sb("h", [P, 2, GG * D])
        hT = sb("hT", [P, 2, GG * N])
        Wh = sb("Wh", [P, 2, GG * D])
        mask = sb("mask", [P, 2, GG * N])
        em = sb("em", [P, GG * N])
        lr = sb("lr", [P, 2, GG * N])
        neg_max = sb("neg_max", [P, 2, GG])
        row_sum = sb("row_sum", [P, 2, GG])
        row_inv = sb("row_inv", [P, GG])
        prob = sb("prob", [P, 2, GG * N])
        probT = sb("probT", [P, GG * N])
        h2 = sb("h2", [P, 2, GG * D])
        h2T = sb("h2T", [P, GG * N])
        TE = TS * NE
        r_m = sb("r_m", [P, 4, TS])
        r_a = sb("r_a", [P, TE])
        r_b = sb("r_b", [P, TE])
        r_l2 = sb("r_l2", [P, TE])
        oh = sb("oh", [P, 2, TE])
        r_e = sb("r_e", [P, 3, TS])
        chosen = sb("chosen", [P, TE], BF16)
        cnt = sb("cnt", [TS, NE], BF16)
        cnt_b = sb("cnt_b", [TS, TE], BF16)
        r_c = sb("r_c", [P, NE, TS])
        r_ee = sb("r_ee", [P, NE, NE])
        r_t = sb("r_t", [P, 4, NE])
        r_row = sb("r_row", [P, 2, TS])
        r_idf = sb("r_idf", [1, NT])
        r_id = sb("r_id", [1, NT, NE - 1])
        xs_t = sb("xs_t", [P, 2, QT, D])
        xT = sb("xT", [P, 2, QT * P])
        sil = sb("sil", [P, 2, HID])
        hid = sb("hid", [P, 2, HID])
        hidT = sb("hidT", [P, 2, HID])
        yo = sb("yo", [P, 2, QT * D])
        got = hT[:].rearrange("p a (b k d) -> p (a b) k d", b=2, d=D)
        part = h[:, 0, :].rearrange("p (a d) -> p a d", d=D)
        res = h[:, 1, :].rearrange("p (a d) -> p a d", d=D)

        bank = [ctx.enter_context(nc.psum_tensor(f"bank{i}", [P, 512], F32)) for i in range(8)]

        loaded = [sem(f"loaded{i}") for i in range(2)]
        small_in = sem("small_in")
        weights_in = sem("weights_in")
        zeroed = [sem(f"zeroed{s}") for s in range(NSEG)]
        consts = sem("consts")
        const_steps = sem("const_steps")
        setup_v = sem("setup_v")
        setup_p = sem("setup_p")
        bn1, bn2, ag1, ag2 = sem("bn1"), sem("bn2"), sem("ag1"), sem("ag2")
        var_ready, rstd_ready = sem("var_ready"), sem("rstd_ready")
        h_ready, h_turned, hT_ready = sem("h_ready"), sem("h_turned"), sem("hT_ready")
        e_done, wh_done, wh_ready = sem("e_done"), sem("wh_done"), sem("wh_ready")
        mask_ready, em_ready, lr_ready = sem("mask_ready"), sem("em_ready"), sem("lr_ready")
        max_ready, exp_done = sem("max_ready"), sem("exp_done")
        prob_turned, probT_ready, att_done = sem("prob_turned"), sem("probT_ready"), sem("att_done")
        inv_ready, x2_ready = sem("inv_ready"), sem("x2_ready")
        h2_kept = [sem(f"h2_kept{i}") for i in range(2)]
        h2_ready, h2_turned, h2T_ready = sem("h2_ready"), sem("h2_turned"), sem("h2T_ready")
        logits_done, logits_ready = sem("logits_done"), sem("logits_ready")
        r_steps, r_diff, r_exp = sem("r_steps"), sem("r_diff"), sem("r_exp")
        r_chosen, r_counted, r_cnt, r_pos = sem("r_chosen"), sem("r_counted"), sem("r_cnt"), sem("r_pos")
        r_read = sem("r_read")
        rows_ready, eid_ready = sem("rows_ready"), sem("eid_ready")
        scattered = [sem(f"scattered{s}") for s in range(NSEG)]
        xs_in, xs_turned, xT_ready = sem("xs_in"), sem("xs_turned"), sem("xT_ready")
        up_done, silu_ready, hid_ready = sem("up_done"), sem("silu_ready"), sem("hid_ready")
        hid_turned, hidT_ready, down_done = sem("hid_turned"), sem("hidT_ready"), sem("down_done")
        yo_ready, y_stored = sem("yo_ready"), sem("y_stored")
        gathered = [sem(f"gathered{i}") for i in range(4)]
        part_ready, res_ready = sem("part_ready"), sem("res_ready")
        out_stored = [sem(f"out_stored{i}") for i in range(2)]

        block = ctx.enter_context(nc.Block())

        C0 = NQ - 1 - 2 * (TS // 4)

        def later(n, least):
            return not isinstance(n, int) or n >= least

        def phases(eng, iteration, route):
            def peeled(i):
                steps = {k: 0 <= i - k < NI for k in range(-1, 5)}
                iteration(i, i % 2, lambda k: steps[k])

            for i in range(6):
                peeled(i)
            with eng.Fori(0, (IS + 4 - 6) // 2) as r:
                i = r * 2 + 6
                iteration(i, 0)
                iteration(i + 1, 1)
            route(0)
            with eng.Fori(0, (NI - 2 - (IS + 4)) // 2) as r:
                i = r * 2 + (IS + 4)
                iteration(i, 0)
                iteration(i + 1, 1)
            for i in range(NI - 2, NI + 4):
                peeled(i)
            route(1)

        x_v = x.rearrange("g n d -> n g d")
        adj_v = adj.rearrange("g n m -> n g m")
        out_v = out.rearrange("g n d -> n g d")

        @block.sync
        def _(sp):
            def load_group(i, par):
                if later(i, 2):
                    sp.wait_ge(mask_ready, i - 1)
                    sp.wait_ge(bn1, i - 1)
                sp.dma_start(X[:, bass.ds(i * GG, GG), :], x_v[:, bass.ds(i * GG, GG), :]).then_inc(loaded[par], 16)
                sp.dma_start(adj_t[:, par, :].rearrange("p (g m) -> p g m", g=GG),
                             adj_v[:, bass.ds(i * GG, GG), :]).then_inc(loaded[par], 16)

            def zero_rows(s, c):
                sp.dma_start(xs[s][bass.ds(c * ZC * P, ZC * P), :].rearrange("(t p) n -> p t n", p=P),
                             zeros[:].rearrange("p (t n) -> p t n", n=D)).then_inc(zeroed[s], 16)

            def keep(k, par):
                sp.wait_ge(h2_ready, k + 1)
                sp.dma_start(H2[:, bass.ds(k * GG, GG), :],
                             h2[:, par, :].rearrange("p (g d) -> p g d", d=D)).then_inc(h2_kept[par], 16)

            w12 = W12[:].rearrange("p (e k h) -> p e k h", e=NE, k=2)

            def load_expert(e):
                for k, w in enumerate((w1, w2)):
                    sp.dma_start(w12[:, bass.ds(e, 1), k, :],
                                 w[bass.ds(e, 1), :, :].rearrange("e d h -> d e h")).then_inc(weights_in, 16)
                sp.dma_start(W3[:, bass.ds(e * (HC * D), HC * D)].rearrange("p (c o) -> p c o", c=HC),
                             w3[bass.ds(e, 1), :, :].rearrange("e (c p) o -> p (e c) o", p=P)).then_inc(weights_in, 16)

            load_group(0, 0)
            sp.dma_start(Wg[:], gnn_w).then_inc(small_in, 16)
            for k in range(2):
                sp.dma_start(a12[:, k:k + 1], gnn_a[k * D:(k + 1) * D, :]).then_inc(small_in, 16)
            sp.dma_start(gw[:], gate_w).then_inc(small_in, 16)
            sp.dma_start(gb[:], gate_b.rearrange("(o e) -> o e", o=1).broadcast_to([P, NE])).then_inc(small_in, 16)
            load_group(1, 1)
            sp.wait_ge(consts, 1)
            for c in range(4):
                load_group(c + 2, c % 2)
                if c == 3:
                    keep(0, 0)
                zero_rows(0, c)
                load_expert(c)
            with sp.Fori(0, (IS - 4) // 2) as r:
                c = r * 2 + 4
                for odd in range(2):
                    load_group(c + odd + 2, odd)
                    keep(c + odd - 3, 1 - odd)
                    zero_rows(0, c + odd)
                    load_expert(c + odd)
            with sp.Fori(0, (NI - 2 - IS) // 2) as r:
                c = r * 2 
                for odd in range(2):
                    load_group(c + odd + IS + 2, odd)
                    keep(c + odd + IS - 3, 1 - odd)
                    zero_rows(1, c + odd)
                    load_expert(c + odd + IS)
            for c in range(NI - 2 - IS, IS):
                zero_rows(1, c)
                load_expert(c + IS)
            for k in range(NI - 5, NI):
                keep(k, k % 2)

            def load_quad(s, n, par):
                if later(n, 2):
                    sp.wait_ge(xs_turned, n - 1)
                if later(n, 1):
                    sp.wait_ge(xs_in, 16 * n)
                sp.dma_start(xs_t[:, par, :, :],
                             xs[s][bass.ds((n - s * QS) * QT * P, QT * P), :].rearrange("(t p) n -> p t n", p=P))\
                  .then_inc(xs_in, 16)

            def store_half(t, half):
                sp.wait_ge(res_ready, t + 2)
                sp.dma_start(out_v[:, bass.ds(t, 2), :], res[:, 2 * half:2 * half + 2, :]).then_inc(out_stored[half], 16)

            sp.wait_ge(scattered[0], 16 * 2 * TS)
            load_quad(0, 0, 0)
            load_quad(0, 1, 1)
            with sp.Fori(0, (QS - 1 - 1) // 2) as r:
                q = r * 2 + 1
                load_quad(0, q + 1, 0)
                load_quad(0, q + 2, 1)
            sp.wait_ge(scattered[1], 16 * 2 * TS)
            with sp.Fori(0, (C0 - (QS - 1)) // 2) as r:
                q = r * 2 + (QS - 1)
                load_quad(1, q + 1, 0)
                load_quad(1, q + 2, 1)
            with sp.Fori(0, (NQ - 1 - C0) // 2) as r:
                q = r * 2 + C0
                load_quad(1, q + 1, 0)
                load_quad(1, q + 2, 1)
                store_half(r * 4, 0)
                store_half(r * 4 + 2, 1)
            with sp.Fori(0, (NG - TS) // 4) as r:
                t = r * 4 + TS
                store_half(t, 0)
                store_half(t + 2, 1)
            for half in range(2):
                sp.wait_ge(out_stored[half], 16 * NG // 4)

        @block.tensor
        def _(pe):
            TH, TP, TH2, E, WH, HP, LO, RT = bank
            pe.wait_ge(small_in, 80)
            pe.wait_ge(const_steps, 9)
            pe.wait_ge(setup_v, 1)
            nc.tensor.transpose(TH[:, 0:P], Wg[:], ident[:])
            nc.tensor.matmul(TH[:, P:2 * P], Wg[:], a12b[:, 0, :], start=True, stop=True)
            nc.tensor.matmul(TH[:, 2 * P:3 * P], Wg[:], a12b[:, 1, :], start=True, stop=True).then_inc(setup_p, 1)
            pe.wait_ge(setup_v, 4)

            def turn(dst, src, last):
                for g in range(GG):
                    ins = nc.tensor.transpose(dst[:, g * P:(g + 1) * P], src(g), ident[:])
                ins.then_inc(last, 1)

            def iteration(i, par, has=lambda k: True):
                if has(2):
                    j = i - 2
                    if later(j, 1):
                        pe.wait_ge(probT_ready, j)
                    pe.wait_ge(exp_done, (j + 1) * GG)
                    turn(TP, lambda g: prob[:, par, g * N:(g + 1) * N], prob_turned)
                if has(4):
                    k = i - 4
                    pe.wait_ge(h2T_ready, k + 1)
                    if later(k, 1):
                        pe.wait_ge(logits_ready, k)
                    for g in range(GG):
                        ins = nc.tensor.matmul(LO[:, g * NE:(g + 1) * NE], h2T[:, g * N:(g + 1) * N], gw[:],
                                               start=True, stop=True)
                    ins.then_inc(logits_done, 1)
                if has(2):
                    pe.wait_ge(probT_ready, j + 1)
                    pe.wait_ge(wh_ready, j + 1)
                    if later(j, 1):
                        pe.wait_ge(x2_ready, j)
                    for g in range(GG):
                        ins = nc.tensor.matmul(HP[:, g * D:(g + 1) * D], probT[:, g * N:(g + 1) * N],
                                               Wh[:, par, g * D:(g + 1) * D], start=True, stop=True)
                    ins.then_inc(att_done, 1)
                if has(0):
                    pe.wait_ge(h_ready, i + 1)
                    if later(i, 1):
                        pe.wait_ge(hT_ready, i)
                    turn(TH, lambda g: h[:, par, g * D:(g + 1) * D], h_turned)
                if has(3):
                    k = i - 3
                    pe.wait_ge(h2_ready, k + 1)
                    if later(k, 1):
                        pe.wait_ge(h2T_ready, k)
                    turn(TH2, lambda g: h2[:, 1 - par, g * D:(g + 1) * D], h2_turned)
                if has(0):
                    pe.wait_ge(hT_ready, i + 1)
                    if later(i, 1):
                        pe.wait_ge(em_ready, i)
                    nc.tensor.matmul(E[:], dst_w[:], hT[:, par, :], start=True, stop=False)
                    for g in range(GG):
                        ins = nc.tensor.matmul(E[:, g * N:(g + 1) * N], hT[:, par, g * N:(g + 1) * N], src_w[:],
                                               start=False, stop=(g == GG - 1))
                    ins.then_inc(e_done, 1)
                    if later(i, 1):
                        pe.wait_ge(wh_ready, i)
                    for g in range(GG):
                        ins = nc.tensor.matmul(WH[:, g * D:(g + 1) * D], hT[:, par, g * N:(g + 1) * N], WgT[:],
                                               start=True, stop=True)
                    ins.then_inc(wh_done, 1)

            def route(s):
                pe.wait_ge(r_chosen, s + 1)
                tab = chosen[:].rearrange("p (t e) -> p t e", e=NE)
                for e in range(NE):
                    ins = nc.tensor.matmul(LO[0:TS, 64 + e:65 + e], tab[:, :, e], ones_bf[:, 0:1], start=True, stop=True)
                ins.then_inc(r_counted, 1)
                pe.wait_ge(r_cnt, 2 * s + 1)
                nc.tensor.matmul(LO[:, 128:128 + NE], ones_bf[0:TS, :], cnt[:], start=True, stop=True)
                pe.wait_ge(r_cnt, 2 * s + 2)
                nc.tensor.matmul(RT[:, 0:TE], before_bf[:], chosen[:], start=True, stop=False)
                nc.tensor.matmul(RT[:, 0:TE], ones_bf[0:TS, :], cnt_b[:], start=False, stop=True).then_inc(r_pos, 1)
                pe.wait_ge(r_read, s + 1)

            phases(pe, iteration, route)

            XP, H0, H1, T0, T1, O0, O1, _ = bank
            H, HT, O = (H0, H1), (T0, T1), (O0, O1)
            pe.wait_ge(weights_in, 48 * NE)
            pe.wait_ge(eid_ready, NSEG)
            pe.wait_ge(rows_ready, NSEG)

            def experts(q):
                _, values = nc.values_load_multi_w_load_instructions(
                    EID[0:1, bass.ds(q * QT, QT)], engines=(mybir.EngineType.PE,), min_val=0, max_val=NE - 1,
                    skip_runtime_bounds_check_because="a count over NE - 1 experts")
                return list(values)

            def turn_rows(q, par):
                pe.wait_ge(xs_in, 16 * (q + 1))
                if later(q, 1):
                    pe.wait_ge(xT_ready, q)
                turn(XP, lambda k: xs_t[:, par, k, :], xs_turned)

            def up(t, k, q, par, e):
                if k == 0:
                    pe.wait_ge(xT_ready, q + 1)
                if later(t, 2):
                    pe.wait_ge(hid_ready, t - 1)
                nc.tensor.matmul(H[k % 2][:, 0:2 * HID], xT[:, par, k * P:(k + 1) * P],
                                 W12[:, bass.ds(e * (2 * HID), 2 * HID)], start=True, stop=True).then_inc(up_done, 1)

            def down(t, k, q, par, e):
                pe.wait_ge(hidT_ready, t + 1)
                if k == 0 and later(q, 2):
                    pe.wait_ge(yo_ready, q - 1)
                for c in range(HC):
                    ins = nc.tensor.matmul(O[par][:, k * D:(k + 1) * D], hidT[:, k % 2, c * P:(c + 1) * P],
                                           W3[:, bass.ds(e * (HC * D) + c * D, D)], start=(c == 0), stop=(c == HC - 1))
                ins.then_inc(down_done, 1)

            def quad(q, par, e, e_last, last=False):
                for k in range(QT):
                    t = q * QT + k
                    if k < QT - 1:
                        up(t + 1, k + 1, q, par, e[k + 1])
                    elif not last:
                        up(t + 1, 0, q + 1, 1 - par, e_next[0])
                    if k == 0:
                        if e_last is not None:
                            down(t - 1, QT - 1, q - 1, 1 - par, e_last)
                        if not last:
                            e_next = experts(q + 1)
                    else:
                        down(t - 1, k - 1, q, par, e[k - 1])
                    if k == 1 and not last:
                        turn_rows(q + 1, 1 - par)
                    pe.wait_ge(hid_ready, t + 1)
                    if later(t, 2):
                        pe.wait_ge(hidT_ready, t - 1)
                    for c in range(HC):
                        ins = nc.tensor.transpose(HT[k % 2][:, c * P:(c + 1) * P], hid[:, k % 2, c * P:(c + 1) * P], ident[:])
                    ins.then_inc(hid_turned, 1)
                if last:
                    down(t, QT - 1, q, par, e[QT - 1])
                    return None, None
                return e_next, e[QT - 1]

            turn_rows(0, 0)
            e = experts(0)
            up(0, 0, 0, 0, e[0])
            e, e_last = quad(0, 0, e, None)
            e, e_last = quad(1, 1, e, e_last)
            quad(2, 0, e, e_last)
            with pe.Fori(0, (NQ - 1 - 3) // 2) as r:
                q = r * 2 + 3
                e_last = experts(q - 1)[QT - 1]
                e, e_last = quad(q, 1, experts(q), e_last)
                quad(q + 1, 0, e, e_last)
            quad(NQ - 1, 1, experts(NQ - 1), experts(NQ - 2)[QT - 1], last=True)

        @block.scalar
        def _(act):
            TH, TP, TH2, E, WH, HP, LO, RT = bank

            def iteration(i, par, has=lambda k: True):
                if has(2):
                    j = i - 2
                    act.wait_ge(prob_turned, j + 1)
                    if later(j, 1):
                        act.wait_ge(att_done, j)
                    nc.scalar.activation(probT[:], TP[:], ACT.Copy).then_inc(probT_ready, 1)
                if has(0):
                    act.wait_ge(loaded[par], 32 * (i // 2) + 32 if isinstance(i, int) else (i - par) * 16 + 32)
                    if later(i, 2):
                        act.wait_ge(em_ready, i - 1)
                    nc.scalar.activation(mask[:, par, :], adj_t[:, par, :], ACT.Relu, scale=2 * MASKED).then_inc(mask_ready, 1)
                if has(1):
                    j = i - 1
                    act.wait_ge(max_ready, j + 1)
                    if later(j, 2):
                        act.wait_ge(prob_turned, j - 1)
                        act.wait_ge(inv_ready, j - 1)
                    for g in range(GG):
                        nc.scalar.activation(prob[:, 1 - par, g * N:(g + 1) * N], lr[:, 1 - par, g * N:(g + 1) * N], ACT.Exp,
                                             bias=neg_max[:, 1 - par, g:g + 1],
                                             accum_out=row_sum[:, 1 - par, g:g + 1]).then_inc(exp_done, 1)
                if has(0):
                    act.wait_ge(h_turned, i + 1)
                    if later(i, 2):
                        act.wait_ge(wh_done, i - 1)
                    nc.scalar.activation(hT[:, par, :], TH[:], ACT.Copy).then_inc(hT_ready, 1)
                if has(3):
                    k = i - 3
                    act.wait_ge(h2_turned, k + 1)
                    if later(k, 1):
                        act.wait_ge(logits_done, k)
                    nc.scalar.activation(h2T[:], TH2[:], ACT.Copy).then_inc(h2T_ready, 1)
                if has(0):
                    act.wait_ge(wh_done, i + 1)
                    if later(i, 2):
                        act.wait_ge(att_done, i - 1)
                    nc.scalar.activation(Wh[:, par, :], WH[:], ACT.Copy).then_inc(wh_ready, 1)

            def route(s):
                act.wait_ge(r_diff, s + 1)
                nc.scalar.activation(r_e[:, 1, :], r_e[:, 0, :], ACT.Exp).then_inc(r_exp, 1)

            phases(act, iteration, route)

            XP, H0, H1, T0, T1, O0, O1, _ = bank
            H, O = (H0, H1), (O0, O1)

            def copy_rows(q, par):
                act.wait_ge(xs_turned, q + 1)
                if later(q, 2):
                    act.wait_ge(up_done, (q - 1) * QT)
                nc.scalar.activation(xT[:, par, :], XP[:], ACT.Copy).then_inc(xT_ready, 1)

            def silu(t, k):
                act.wait_ge(up_done, t + 1)
                if later(t, 2):
                    act.wait_ge(hid_ready, t - 1)
                nc.scalar.activation(sil[:, k % 2, :], H[k % 2][:, 0:HID], ACT.Silu).then_inc(silu_ready, 1)

            def copy_out(q, par):
                act.wait_ge(down_done, (q + 1) * QT)
                if later(q, 2):
                    act.wait_ge(y_stored, 16 * (q - 1))
                nc.scalar.activation(yo[:, par, :], O[par][:], ACT.Copy).then_inc(yo_ready, 1)

            def store_out(s, q, par):
                act.wait_ge(yo_ready, q + 1)
                if later(q, 1):
                    act.wait_ge(y_stored, 16 * q)
                act.dma_start(ys[s][bass.ds((q - s * QS) * QT * P, QT * P), :].rearrange("(t p) n -> p t n", p=P),
                              yo[:, par, :].rearrange("p (t n) -> p t n", n=D)).then_inc(y_stored, 16)

            def quad(q, par, s_prev, first=False, last=False):
                for k in range(QT):
                    if not (last and k == QT - 1):
                        silu(q * QT + k + 1, k + 1)
                    if k == 1 and not last:
                        copy_rows(q + 1, 1 - par)
                    if k == 2 and not first:
                        copy_out(q - 1, 1 - par)
                    if k == 3 and not first:
                        store_out(s_prev, q - 1, 1 - par)

            copy_rows(0, 0)
            silu(0, 0)
            quad(0, 0, 0, first=True)
            quad(1, 1, 0)
            quad(2, 0, 0)
            with act.Fori(0, (QS + 1 - 3) // 2) as r:
                q = r * 2 + 3
                quad(q, 1, 0)
                quad(q + 1, 0, 0)
            with act.Fori(0, (NQ - 1 - (QS + 1)) // 2) as r:
                q = r * 2 + (QS + 1)
                quad(q, 1, 1)
                quad(q + 1, 0, 1)
            quad(NQ - 1, 1, 1, last=True)
            copy_out(NQ - 1, 1)
            store_out(1, NQ - 1, 1)

        @block.vector
        def _(dve):
            TH, TP, TH2, E, WH, HP, LO, RT = bank
            V = nc.vector
            dve.wait_ge(small_in, 80)
            for k in range(2):
                ins = V.tensor_copy(a12b[:, k, :], a12[:, k:k + 1].broadcast_to([P, P]))
            ins.then_inc(setup_v, 1)
            dve.wait_ge(setup_p, 1)
            V.tensor_copy(WgT[:], TH[:, 0:P]).then_inc(setup_v, 1)
            V.tensor_copy(src_w[:], TH[:, P:2 * P]).then_inc(setup_v, 1)
            V.tensor_copy(dst_w[:], TH[:, 2 * P:3 * P]).then_inc(setup_v, 1)

            def carry():
                dve.wait_ge(const_steps, 10)

            def row(t, i, g):
                return t[:, bass.ds(i * GG + g, 1), :].rearrange("p a d -> p (a d)")

            def stats_of(i, batch_par, col, bn):
                for g in range(GG):
                    ins = V.bn_stats(stats[:, batch_par, col + g, :], row(X, i, g))
                ins.then_inc(bn, 1)

            def aggregate(batch_par, col, ag):
                for g in range(GG):
                    V.bn_aggr(mv[:, batch_par, col + g, :], stats[:, batch_par, col + g, :]).then_inc(ag, 1)

            def normalize(i, dst, col, batch_par):
                for g in range(GG):
                    ins = V.tensor_scalar(dst(g), row(X, i, g), mv[:, batch_par, col + g, 0:1],
                                          rstd[:, batch_par, col + g:col + g + 1], ALU.subtract, ALU.mult)
                return ins

            def first_stats(i, par):
                dve.wait_ge(loaded[par], 32 * (i // 2) + 32 if isinstance(i, int) else (i - par) * 16 + 32)
                return i

            def iteration(i, par, has=lambda k: True):
                if has(1):
                    j = i - 1
                    dve.wait_ge(e_done, j + 1)
                    dve.wait_ge(mask_ready, j + 1)
                    if later(j, 1):
                        dve.wait_ge(lr_ready, j)
                    V.scalar_tensor_tensor(em[:], mask[:, 1 - par, :], -MASKED, E[:], ALU.add, ALU.min).then_inc(em_ready, 1)
                    dve.wait_ge(em_ready, j + 1)
                    if later(j, 2):
                        dve.wait_ge(exp_done, (j - 1) * GG)
                    V.scalar_tensor_tensor(lr[:, 1 - par, :], em[:], SLOPE, em[:], ALU.mult, ALU.max).then_inc(lr_ready, 1)
                    dve.wait_ge(lr_ready, j + 1)
                    V.tensor_reduce(neg_max[:, 1 - par, :], lr[:, 1 - par, :].rearrange("p (g m) -> p g m", m=N), AX.X, ALU.max,
                                    negate=True).then_inc(max_ready, 1)
                if has(0) or has(3):
                    dve.wait_ge(rstd_ready, i + 1)
                if has(0):
                    if later(i, 2):
                        dve.wait_ge(h_turned, i - 1)
                    normalize(i, lambda g: h[:, par, g * D:(g + 1) * D], 0, 1 - par).then_inc(h_ready, 1)
                if has(3):
                    k = i - 3
                    if later(k, 2):
                        dve.wait_ge(h2_turned, k - 1)
                        dve.wait_ge(h2_kept[1 - par], k // 2 * 16 if isinstance(k, int) else (k - (1 - par)) * 8)
                    normalize(k, lambda g: h2[:, 1 - par, g * D:(g + 1) * D], GG, 1 - par).then_inc(h2_ready, 1)
                if has(2):
                    j = i - 2
                    dve.wait_ge(exp_done, (j + 1) * GG)
                    V.reciprocal(row_inv[:], row_sum[:, par, :]).then_inc(inv_ready, 1)
                if has(-1):
                    carry()
                    first_stats(i + 1, 1 - par)
                    stats_of(i + 1, par, 0, bn1)
                if has(2):
                    dve.wait_ge(inv_ready, j + 1)
                    dve.wait_ge(att_done, j + 1)
                    for g in range(GG):
                        ins = V.scalar_tensor_tensor(row(X, j, g), HP[:, g * D:(g + 1) * D], row_inv[:, g:g + 1],
                                                     row(X, j, g), ALU.mult, ALU.add)
                    ins.then_inc(x2_ready, 1)
                    carry()
                    dve.wait_ge(x2_ready, j + 1)
                    stats_of(j, par, GG, bn2)
                if has(-1):
                    dve.wait_ge(bn1, i + 2)
                if has(2):
                    dve.wait_ge(bn2, j + 1)
                if has(4):
                    k = i - 4
                    dve.wait_ge(logits_done, k + 1)
                    V.tensor_tensor(LG[:, bass.ds(k * GG, GG), :], LO[:, 0:GG * NE].rearrange("p (g e) -> p g e", e=NE),
                                    gb[:].rearrange("p (o e) -> p o e", o=1).broadcast_to([P, GG, NE]), ALU.add)\
                        .then_inc(logits_ready, 1)
                if has(-1):
                    aggregate(par, 0, ag1)
                if has(2):
                    aggregate(par, GG, ag2)
                lo, hi = (0 if has(-1) else GG), (2 * GG if has(2) else GG)
                if hi > lo:
                    if has(-1):
                        dve.wait_ge(ag1, (i + 2) * GG)
                    if has(2):
                        dve.wait_ge(ag2, (i - 1) * GG)
                    V.tensor_scalar(var_eps[:, par, lo:hi], mv[:, par, lo:hi, 1], EPS, None, ALU.add).then_inc(var_ready, 1)

            steps = [0]

            def link(ins):
                steps[0] += 1
                ins.then_inc(r_steps, 1)
                dve.wait_ge(r_steps, steps[0])

            def te(ap):
                return ap.rearrange("p (t e) -> p t e", e=NE)

            def route(s):
                def per_tile(ap):
                    return ap.rearrange("p (t o) -> p t o", o=1).broadcast_to([P, TS, NE])

                def per_expert(ap, n):
                    return ap.rearrange("p (o e) -> p o e", o=1).broadcast_to([P, n, NE])

                dve.wait_ge(logits_ready, (s + 1) * IS)
                logits = LG[:, s * TS:(s + 1) * TS, :]
                for c in range(2):
                    L = logits if c == 0 else te(r_l2[:])
                    link(V.tensor_reduce(r_m[:, c, :], L, AX.X, ALU.max))
                    link(V.tensor_tensor(te(r_a[:]), L, per_tile(r_m[:, c, :]), ALU.is_equal))
                    link(V.tensor_tensor(te(r_b[:]), te(r_a[:]), per_expert(e_rank[:], TS), ALU.mult))
                    link(V.tensor_reduce(r_m[:, 2 + c, :], te(r_b[:]), AX.X, ALU.max))
                    link(V.tensor_tensor(te(oh[:, c, :]), te(r_b[:]), per_tile(r_m[:, 2 + c, :]), ALU.is_equal))
                    if c == 0:
                        link(V.scalar_tensor_tensor(r_l2[:], oh[:, 0, :], -3e38,
                                                    logits.rearrange("p t e -> p (t e)"), ALU.mult, ALU.add))
                V.tensor_tensor(chosen[:], oh[:, 0, :], oh[:, 1, :], ALU.add).then_inc(r_chosen, 1)
                V.tensor_tensor(r_e[:, 0, :], r_m[:, 1, :], r_m[:, 0, :], ALU.subtract).then_inc(r_diff, 1)
                dve.wait_ge(r_counted, s + 1)
                V.tensor_copy(cnt[:], LO[0:TS, 64:64 + NE]).then_inc(r_cnt, 1)
                dve.wait_ge(r_cnt, 2 * s + 1)
                V.tensor_tensor(te(cnt_b[:]),
                                before[0:TS, 0:TS].rearrange("p (t o) -> p t o", o=1).broadcast_to([TS, TS, NE]),
                                cnt[:].rearrange("p (o e) -> p o e", o=1).broadcast_to([TS, TS, NE]), ALU.mult).then_inc(r_cnt, 1)
                gates = GATE[:, :, s * TS:(s + 1) * TS]
                dve.wait_ge(r_exp, s + 1)
                link(V.tensor_scalar(r_e[:, 2, :], r_e[:, 1, :], 1.0, None, ALU.add))
                link(V.reciprocal(gates[:, 0, :], r_e[:, 2, :]))
                link(V.tensor_tensor(gates[:, 1, :], r_e[:, 1, :], gates[:, 0, :], ALU.mult))
                dve.wait_ge(r_pos, s + 1)
                total = LO[:, 128:128 + NE]
                V.tensor_tensor(r_c[:], total.rearrange("p (e o) -> p e o", o=1).broadcast_to([P, NE, TS]),
                                     tile_rows[:].rearrange("p (o j) -> p o j", o=1).broadcast_to([P, NE, TS]), ALU.is_gt).then_inc(r_read, 1)
                dve.wait_ge(r_read, s + 1)
                link(V.tensor_reduce(r_t[:, 0, :], r_c[:], AX.X, ALU.add))
                link(V.tensor_tensor(r_ee[:], e_before[:], per_expert(r_t[:, 0, :], NE), ALU.mult))
                link(V.tensor_reduce(r_t[:, 1, :], r_ee[:], AX.X, ALU.add))
                link(V.tensor_scalar(r_t[:, 3, :], r_t[:, 1, :], float(P), None, ALU.mult))
                link(V.tensor_tensor(te(r_a[:]), te(RT[:, 0:TE]), per_expert(r_t[:, 3, :], TS), ALU.add))
                for c in range(2):
                    link(V.tensor_tensor(r_b[:], oh[:, c, :], r_a[:], ALU.mult))
                    link(V.tensor_reduce(r_row[:, c, :], te(r_b[:]), AX.X, ALU.add))
                link(V.tensor_tensor(r_t[:, 2, :], r_t[:, 1, :], r_t[:, 0, :], ALU.add))
                V.tensor_copy(ROW[:, s, :, :], r_row[:]).then_inc(rows_ready, 1)
                dve.wait_ge(rows_ready, s + 1)
                link(V.tensor_tensor(r_id[:], r_t[0:1, 2, 0:NE - 1].rearrange("p (o e) -> p o e", o=1).broadcast_to([1, NT, NE - 1]),
                                     tile_no[:].rearrange("p (j o) -> p j o", o=1).broadcast_to([1, NT, NE - 1]), ALU.is_le))
                link(V.tensor_reduce(r_idf[:], r_id[:], AX.X, ALU.add))
                V.tensor_copy(EID[0:1, s * NT:(s + 1) * NT], r_idf[:]).then_inc(eid_ready, 1)

            dve.wait_ge(const_steps, 10)
            first_stats(0, 0)
            stats_of(0, 1, 0, bn1)
            dve.wait_ge(bn1, 1)
            aggregate(1, 0, ag1)
            dve.wait_ge(ag1, GG)
            V.tensor_scalar(var_eps[:, 1, 0:GG], mv[:, 1, 0:GG, 1], EPS, None, ALU.add).then_inc(var_ready, 1)
            phases(dve, iteration, route)

            XP, H0, H1, T0, T1, O0, O1, _ = bank
            H, HT = (H0, H1), (T0, T1)

            def gate_hidden(t, k):
                dve.wait_ge(silu_ready, t + 1)
                if later(t, 2):
                    dve.wait_ge(hid_turned, t - 1)
                V.tensor_tensor(hid[:, k % 2, :], sil[:, k % 2, :], H[k % 2][:, HID:2 * HID], ALU.mult).then_inc(hid_ready, 1)

            def quad(q, last=False):
                for k in range(QT):
                    t = q * QT + k
                    dve.wait_ge(hid_turned, t + 1)
                    if later(t, 2):
                        dve.wait_ge(down_done, t - 1)
                    V.tensor_copy(hidT[:, k % 2, :], HT[k % 2][:, 0:HID]).then_inc(hidT_ready, 1)
                    if not (last and k == QT - 1):
                        gate_hidden(t + 1, k + 1)

            def combine(t, slot, first):
                dve.wait_ge(gathered[slot], t * 8 + (32 - 8 * slot))
                def weight(c):
                    return GATE[:, c, bass.ds(t, 1)]
                V.scalar_tensor_tensor(part[:, slot, :], got[:, slot, 0, :], weight(0),
                                       X[:, bass.ds(t, 1), :].rearrange("p a d -> p (a d)"), ALU.mult, ALU.add)\
                    .then_inc(part_ready, 1)
                if not first:
                    dve.wait_ge(out_stored[slot // 2], t * 4 - 4 * slot)
                dve.wait_ge(part_ready, t + 1)
                V.scalar_tensor_tensor(res[:, slot, :], got[:, slot, 1, :], weight(1), part[:, slot, :],
                                       ALU.mult, ALU.add).then_inc(res_ready, 1)

            gate_hidden(0, 0)
            for q in range(3):
                quad(q)
            with dve.Fori(0, (C0 - 3) // 2) as r:
                q = r * 2 + 3
                quad(q)
                quad(q + 1)

            def with_combine(q, t, first):
                quad(q)
                combine(t, 0, first)
                combine(t + 1, 1, first)
                quad(q + 1)
                combine(t + 2, 2, first)
                combine(t + 3, 3, first)
            with_combine(C0, 0, True)
            with dve.Fori(0, (NQ - 1 - (C0 + 2)) // 2) as r:
                q = r * 2 + (C0 + 2)
                with_combine(q, r * 4 + 4, False)
            quad(NQ - 1, last=True)
            with dve.Fori(0, (NG - TS) // 4) as r:
                t = r * 4 + TS
                for slot in range(4):
                    combine(t + slot, slot, False)

        @block.gpsimd
        def _(pool):
            g = nc.gpsimd
            g.memset(zeros[:], 0.0).then_inc(consts, 1)
            g.memset(half_neg[:], -0.5).then_inc(const_steps, 1)
            g.memset(ident[:], 0.0).then_inc(const_steps, 1)
            g.memset(before[:], 1.0).then_inc(const_steps, 1)
            g.memset(ones_bf[:], 1.0).then_inc(const_steps, 1)
            g.memset(e_before[:], 1.0).then_inc(const_steps, 1)
            pool.wait_ge(const_steps, 5)
            g.affine_select(out=ident[:], in_=ident[:], compare_op=ALU.not_equal, fill=1.0, base=0,
                            pattern=[[-1, P]], channel_multiplier=1).then_inc(const_steps, 1)
            g.affine_select(out=before[:], in_=before[:], compare_op=ALU.is_gt, fill=0.0, base=0,
                            pattern=[[1, P]], channel_multiplier=-1).then_inc(const_steps, 1)
            g.affine_select(out=e_before[:], in_=e_before[:], compare_op=ALU.is_gt, fill=0.0, base=0,
                            pattern=[[1, NE], [-1, NE]], channel_multiplier=0).then_inc(const_steps, 1)
            pool.wait_ge(const_steps, 8)
            g.tensor_copy(before_bf[:], before[:]).then_inc(const_steps, 1)
            g.iota(e_rank[:], pattern=[[-1, NE]], base=NE, channel_multiplier=0, allow_small_or_imprecise_dtypes=True)
            g.iota(tile_rows[:], pattern=[[P, TS]], base=0, channel_multiplier=0, allow_small_or_imprecise_dtypes=True)
            g.iota(tile_no[:], pattern=[[1, NT]], base=0, channel_multiplier=0, allow_small_or_imprecise_dtypes=True).then_inc(const_steps, 1)

            def root(i):
                par = i % 2
                lo, hi = (0 if i + 1 < NI else GG), (2 * GG if i >= 2 else GG)
                pool.wait_ge(var_ready, i + 2)
                if i >= 1:
                    pool.wait_ge(h_ready, min(i, NI))
                if i >= 4:
                    pool.wait_ge(h2_ready, i - 3)
                g.tensor_tensor(rstd[:, par, lo:hi], var_eps[:, par, lo:hi], half_neg[:, lo:hi], ALU.pow).then_inc(rstd_ready, 1)

            def scatter(s, n):
                t, c = n // 2, n % 2
                pool.indirect_dma_start(xs[s], bass.IndirectOffsetOnAxis(ap=ROW[:, s, c, t:t + 1], axis=0),
                                        H2[:, s * TS + t, :], None).then_inc(scattered[s], 16)

            n = 0
            for i in range(-1, NI + 2):
                root(i)
                if i == IS + 4:
                    pool.wait_ge(zeroed[0], 16 * IS)
                    pool.wait_ge(rows_ready, 1)
                    for par in range(2):
                        pool.wait_ge(h2_kept[par], 8 * IS)
                if i >= IS + 4:
                    for _ in range(6):
                        scatter(0, n)
                        n += 1
            for m in range(n, 2 * TS):
                scatter(0, m)
            pool.wait_ge(zeroed[1], 16 * IS)
            pool.wait_ge(rows_ready, 2)
            for par in range(2):
                pool.wait_ge(h2_kept[par], 8 * NI)
            for m in range(2 * TS):
                scatter(1, m)
            for s in range(NSEG):
                pool.wait_ge(y_stored, 16 * QS * (s + 1))
                for t in range(TS):
                    n = s * TS + t
                    if n >= 4:
                        pool.wait_ge(res_ready, n - 3)
                    for c in range(2):
                        pool.indirect_dma_start(got[:, n % 4, c, :], None, ys[s],
                                                bass.IndirectOffsetOnAxis(ap=ROW[:, s, c, t:t + 1], axis=0))\
                            .then_inc(gathered[n % 4], 16)


_INS = ['x', 'adj', 'L0_gnn_W', 'L0_gnn_a', 'L0_ffn_gate_w', 'L0_ffn_gate_b', 'L0_ffn_w1', 'L0_ffn_w2', 'L0_ffn_w3']
_OUTS = [((64, 128, 128), 'float32')]


def kernel(**inputs):
    import numpy as _np
    import concourse.bacc as _bacc
    from concourse import mybir as _mybir
    from concourse.bass_utils import run_bass_kernel_spmd as _run

    nc = _bacc.Bacc("TRN2", target_bir_lowering=False, num_devices=1)
    arrays, args = {}, []
    for name in _INS:
        a = _np.ascontiguousarray(inputs[name])
        arrays[f"in_{name}_dram"] = a
        args.append(nc.dram_tensor(f"in_{name}_dram", a.shape, _mybir.dt.from_np(a.dtype), kind="ExternalInput").ap())
    for i, (shape, dtype) in enumerate(_OUTS):
        dt = _mybir.dt.from_np(_np.dtype(dtype))
        args.append(nc.dram_tensor(f"out_{i}_dram", shape, dt, kind="ExternalOutput").ap())
    gat_moe_kernel(nc, *args)
    r = _run(nc, [arrays], core_ids=[0])
    return r.results[0]["out_0_dram"]
```

```python
import concourse.bass as bass
from concourse import mybir
from contextlib import ExitStack

F32 = mybir.dt.float32
BF16 = mybir.dt.bfloat16
I32 = mybir.dt.int32
U32 = mybir.dt.uint32
ALU = mybir.AluOpType
ACT = mybir.ActivationFunctionType
AX = mybir.AxisListType


def gat_moe_kernel(nc: bass.Bass, x, adj, gnn_w, gnn_a, gate_w, gate_b, w1, w2, w3, out):
    NG, N, D = x.shape
    P = 128
    assert N == P and D == P
    GG = 4
    NI = NG // GG
    NE = gate_w.shape[1]
    HID = w1.shape[2]
    HC = HID // P
    SLOPE, EPS = 0.2, 1e-5
    MASKED = 9e15 / SLOPE
    NSEG = 2
    TS = NG // NSEG
    IS = NI // NSEG
    QT = 4
    NT = -(-(2 * TS + NE - 1) // QT) * QT
    QS = NT // QT
    NQ = NSEG * QS
    ZC = NT // IS
    assert ZC * IS == NT

    DW = D + 1
    YB = 8
    CG = TS // QT
    CB = NQ - 3 * CG // 2
    assert CB % 2 == 0 and CB < NQ - YB

    xs = [nc.dram_tensor(f"sorted_rows{s}", (NT * P, DW), F32, kind="Internal").ap() for s in range(NSEG)]
    ys = [nc.dram_tensor(f"token_rows{s}", ((NT + 2 * TS) * P, D), F32, kind="Internal").ap() for s in range(NSEG)]

    ctx = ExitStack()
    with ctx:
        def sb(name, shape, dt=F32):
            return ctx.enter_context(nc.sbuf_tensor(name, shape, dt))

        def sem(name):
            return ctx.enter_context(nc.semaphore(name))

        X = sb("X", [P, NG, D])
        H2 = sb("H2", [P, NG, DW])
        DEST = sb("DEST", [P, NQ * QT], U32)
        W12 = sb("W12", [P, NE * 2 * HID])
        W3 = sb("W3", [P, NE * HC * D])
        LG = sb("LG", [P, NG, NE])
        GATE = sb("GATE", [P, 2, NG])
        ROW = sb("ROW", [P, NSEG, 2, TS], U32)
        EID = sb("EID", [1, NSEG * NT], I32)
        ident = sb("ident", [P, P])
        before = sb("before", [P, P])
        before_bf = sb("before_bf", [P, P], BF16)
        ones_bf = sb("ones_bf", [P, P], BF16)
        e_before = sb("e_before", [P, NE, NE])
        e_rank = sb("e_rank", [P, NE])
        tile_no = sb("tile_no", [1, NT])
        half_neg = sb("half_neg", [P, GG])
        zeros = sb("zeros", [P, ZC, DW])
        Wg = sb("Wg", [P, D])
        a12 = sb("a12", [P, 2])
        a12b = sb("a12b", [P, 2, P])
        WgT = sb("WgT", [P, P])
        src_w = sb("src_w", [P, P])
        dst_w = sb("dst_w", [P, P])
        gw = sb("gw", [P, NE])
        gb = sb("gb", [P, NE])
        shared = sb("shared", [P, YB, GG * N])
        mask, lr, Wh = shared[:, 0:2, :], shared[:, 2:4, :], shared[:, 4:6, :]
        adj_t = shared[:, 6:8, :].bitcast(I32)
        stats = sb("stats", [P, 2, 2 * GG, 6])
        mv = sb("mv", [P, 2, 2 * GG, 2])
        var_eps = sb("var_eps", [P, 2, 2 * GG])
        rstd = sb("rstd", [P, 2, 2 * GG])
        shift = sb("shift", [P, 2, GG])
        h = sb("h", [P, 2, GG * D])
        hT = sb("hT", [P, 2, GG * N])
        em = sb("em", [P, GG * N])
        neg_max = sb("neg_max", [P, 2, GG])
        row_sum = sb("row_sum", [P, 2, GG])
        row_inv = sb("row_inv", [P, GG])
        prob = sb("prob", [P, 2, GG * N])
        probT = sb("probT", [P, GG * N])
        h2 = sb("h2", [P, 2, GG * D])
        h2T = sb("h2T", [P, GG * N])
        TE = TS * NE
        r_m = sb("r_m", [P, 4, TS])
        r_a = sb("r_a", [P, TE])
        r_b = sb("r_b", [P, TE])
        r_l2 = sb("r_l2", [P, TE])
        oh = sb("oh", [P, 2, TE])
        r_e = sb("r_e", [P, 3, TS])
        chosen = sb("chosen", [P, TE], BF16)
        cnt = sb("cnt", [TS, NE], BF16)
        cnt_b = sb("cnt_b", [TS, TE], BF16)
        r_c = sb("r_c", [P, NE])
        r_cr = sb("r_cr", [P, NE])
        r_ee = sb("r_ee", [P, NE, NE])
        r_t = sb("r_t", [P, 4, NE])
        r_row = sb("r_row", [P, 2, TS])
        r_idf = sb("r_idf", [1, NT])
        r_id = sb("r_id", [1, NT, NE - 1])
        xs_t = sb("xs_t", [P, 2, QT, DW])
        xT = sb("xT", [P, 2, QT * P])
        sil = em[:].rearrange("p (k m) -> p k m", m=HC * P)
        w_t = sb("w_t", [P, QT, 2 * HID])
        hidT = prob[:].rearrange("p a (k m) -> p (a k) m", m=HC * P)
        yo = shared
        got = [b.rearrange("p a (k c d) -> p (a k) c d", c=2, d=D)
               for b in (hT[:], h2[:], shared[:, 0:2, :], shared[:, 2:4, :])]
        res, part = ([b.rearrange("p (k d) -> p k d", d=D) for b in bs]
                     for bs in ((h[:, 0, :], h[:, 1, :], shared[:, 4, :], shared[:, 5, :]),
                                (probT[:], h2T[:], shared[:, 6, :], shared[:, 7, :])))

        bank = [ctx.enter_context(nc.psum_tensor(f"bank{i}", [P, 512], F32)) for i in range(8)]

        loaded = [sem(f"loaded{i}") for i in range(2)]
        small_in = sem("small_in")
        weights_in = sem("weights_in")
        zeroed = [sem(f"zeroed{s}") for s in range(NSEG)]
        consts = sem("consts")
        const_steps = sem("const_steps")
        setup_v = sem("setup_v")
        setup_p = sem("setup_p")
        bn1, bn2, ag1, ag2 = sem("bn1"), sem("bn2"), sem("ag1"), sem("ag2")
        var1_ready, rstd1_ready = sem("var1_ready"), sem("rstd1_ready")
        var2_ready, rstd2_ready = sem("var2_ready"), sem("rstd2_ready")
        h_ready, h_turned, hT_ready = sem("h_ready"), sem("h_turned"), sem("hT_ready")
        e_done, wh_done, wh_ready = sem("e_done"), sem("wh_done"), sem("wh_ready")
        mask_ready, em_ready, lr_ready = sem("mask_ready"), sem("em_ready"), sem("lr_ready")
        max_ready, exp_done = sem("max_ready"), sem("exp_done")
        prob_turned, probT_ready, att_done = sem("prob_turned"), sem("probT_ready"), sem("att_done")
        inv_ready, x2_ready, shift_ready = sem("inv_ready"), sem("x2_ready"), sem("shift_ready")
        h2_kept = [sem(f"h2_kept{i}") for i in range(2)]
        h2_ready, h2_turned, h2T_ready = sem("h2_ready"), sem("h2_turned"), sem("h2T_ready")
        logits_done, logits_ready = sem("logits_done"), sem("logits_ready")
        r_steps, r_diff, r_exp = sem("r_steps"), sem("r_diff"), sem("r_exp")
        r_chosen, r_counted, r_cnt, r_pos = sem("r_chosen"), sem("r_counted"), sem("r_cnt"), sem("r_pos")
        r_total, r_read = sem("r_total"), sem("r_read")
        rows_ready, eid_ready = sem("rows_ready"), sem("eid_ready")
        scattered = [sem(f"scattered{s}") for s in range(NSEG)]
        xs_in, xs_turned, xT_ready = sem("xs_in"), sem("xs_turned"), sem("xT_ready")
        up_done, silu_ready, hid_ready = sem("up_done"), sem("silu_ready"), sem("hid_ready")
        down_done = sem("down_done")
        w_in = [sem(f"w_in{k}") for k in range(QT)]
        yo_ready, dest_ready, dest_steps = sem("yo_ready"), sem("dest_ready"), sem("dest_steps")
        y_sent = [sem(f"y_sent{i}") for i in range(YB)]
        y_in = [sem(f"y_in{i}") for i in range(4)]
        part_ready, res_ready = sem("part_ready"), sem("res_ready")
        out_stored = [sem(f"out_stored{i}") for i in range(4)]

        block = ctx.enter_context(nc.Block())

        def later(n, least):
            return not isinstance(n, int) or n >= least

        def phases(eng, iteration, route):
            def peeled(i):
                steps = {k: 0 <= i - k < NI for k in range(-1, 5)}
                iteration(i, i % 2, lambda k: steps[k])

            for i in range(6):
                peeled(i)
            with eng.Fori(0, (IS + 4 - 6) // 2) as r:
                i = r * 2 + 6
                iteration(i, 0)
                iteration(i + 1, 1)
            route(0)
            with eng.Fori(0, (NI - 2 - (IS + 4)) // 2) as r:
                i = r * 2 + (IS + 4)
                iteration(i, 0)
                iteration(i + 1, 1)
            for i in range(NI - 2, NI + 4):
                peeled(i)
            route(1)

        def experts(engine, q):
            _, values = nc.values_load_multi_w_load_instructions(
                EID[0:1, bass.ds(q * QT, QT)], engines=(engine,), min_val=0, max_val=NE - 1,
                skip_runtime_bounds_check_because="a count over NE - 1 experts")
            return list(values)

        def group_beside(q):
            n = q - CB
            return 2 * (n // 3) + n % 3 if n >= 0 and n % 3 < 2 else None

        x_v = x.rearrange("g n d -> n g d")
        adj_v = adj.rearrange("g n m -> n g m")
        out_v = out.rearrange("g n d -> n g d")

        @block.sync
        def _(sp):
            def load_group(i, par):
                if later(i, 2):
                    sp.wait_ge(mask_ready, i - 1)
                    sp.wait_ge(bn1, i - 1)
                sp.dma_start(X[:, bass.ds(i * GG, GG), :], x_v[:, bass.ds(i * GG, GG), :]).then_inc(loaded[par], 16)
                sp.dma_start(adj_t[:, par, :].rearrange("p (g m) -> p g m", g=GG),
                             adj_v[:, bass.ds(i * GG, GG), :]).then_inc(loaded[par], 16)

            def zero_rows(s, c):
                sp.dma_start(xs[s][bass.ds(c * ZC * P, ZC * P), :].rearrange("(t p) n -> p t n", p=P), zeros[:]).then_inc(zeroed[s], 16)

            def keep(k, par):
                sp.wait_ge(h2_ready, k + 1)
                sp.dma_start(H2[:, bass.ds(k * GG, GG), 0:D],
                             h2[:, par, :].rearrange("p (g d) -> p g d", d=D)).then_inc(h2_kept[par], 16)

            w12 = W12[:].rearrange("p (e k h) -> p e k h", e=NE, k=2)

            def load_expert(e):
                for k, w in enumerate((w1, w2)):
                    sp.dma_start(w12[:, bass.ds(e, 1), k, :],
                                 w[bass.ds(e, 1), :, :].rearrange("e d h -> d e h")).then_inc(weights_in, 16)
                sp.dma_start(W3[:, bass.ds(e * (HC * D), HC * D)].rearrange("p (c o) -> p c o", c=HC),
                             w3[bass.ds(e, 1), :, :].rearrange("e (c p) o -> p (e c) o", p=P)).then_inc(weights_in, 16)

            load_group(0, 0)
            sp.dma_start(Wg[:], gnn_w).then_inc(small_in, 16)
            for k in range(2):
                sp.dma_start(a12[:, k:k + 1], gnn_a[k * D:(k + 1) * D, :]).then_inc(small_in, 16)
            sp.dma_start(gw[:], gate_w).then_inc(small_in, 16)
            sp.dma_start(gb[:], gate_b.rearrange("(o e) -> o e", o=1).broadcast_to([P, NE])).then_inc(small_in, 16)
            load_group(1, 1)
            sp.wait_ge(consts, 1)
            for c in range(4):
                load_group(c + 2, c % 2)
                if c == 3:
                    keep(0, 0)
                zero_rows(0, c)
                load_expert(c)
            with sp.Fori(0, (IS - 4) // 2) as r:
                c = r * 2 + 4
                for odd in range(2):
                    load_group(c + odd + 2, odd)
                    keep(c + odd - 3, 1 - odd)
                    zero_rows(0, c + odd)
                    load_expert(c + odd)
            with sp.Fori(0, (NI - 2 - IS) // 2) as r:
                c = r * 2 
                for odd in range(2):
                    load_group(c + odd + IS + 2, odd)
                    keep(c + odd + IS - 3, 1 - odd)
                    zero_rows(1, c + odd)
                    load_expert(c + odd + IS)
            for c in range(NI - 2 - IS, IS):
                zero_rows(1, c)
                load_expert(c + IS)
            for k in range(NI - 5, NI):
                keep(k, k % 2)

            def load_quad(s, n, par):
                if later(n, 2):
                    sp.wait_ge(xs_turned, n - 1)
                    sp.wait_ge(dest_ready, n - 1)
                if later(n, 1):
                    sp.wait_ge(xs_in, 16 * n)
                sp.dma_start(xs_t[:, par, :, :],
                             xs[s][bass.ds((n - s * QS) * QT * P, QT * P), :].rearrange("(t p) n -> p t n", p=P))\
                  .then_inc(xs_in, 16)

            def load_results(s, j, b, after=None):
                if after is not None:
                    sp.wait_ge(res_ready, after + 1)
                sp.dma_start(got[b].rearrange("p k c d -> p k (c d)"),
                             ys[s][bass.ds((j - s * CG) * (QT * 2 * P) + NT * P, QT * 2 * P), :]
                             .rearrange("(k p c) d -> p k (c d)", p=P, c=2)).then_inc(y_in[b], 16)

            def store_group(j, b):
                sp.wait_ge(res_ready, j + 1)
                sp.dma_start(out_v[:, bass.ds(j * QT, QT), :], res[b]).then_inc(out_stored[b], 16)

            def results_there(s):
                for b in range(YB):
                    sp.wait_ge(y_sent[b], 16 * QT * len(range(b, QS * (s + 1), YB)))

            def load_up(q, after_third=None):
                for k, e in enumerate(experts(mybir.EngineType.SP, q)):
                    if later(q, 1):
                        sp.wait_ge(up_done, q * QT + k - (QT - 1))
                    sp.dma_start(w_t[:, k, :], W12[:, bass.ds(e * (2 * HID), 2 * HID)]).then_inc(w_in[k], 16)
                    if k == 2 and after_third is not None:
                        after_third()

            def loads(n, s, par, after_third=None):
                load_quad(s, n + 2, par)
                load_up(n + 1, after_third)

            sp.wait_ge(weights_in, 48 * NE)
            sp.wait_ge(eid_ready, 1)
            load_up(0)
            sp.wait_ge(scattered[0], 16 * 2 * TS)
            load_quad(0, 0, 0)
            load_quad(0, 1, 1)
            with sp.Fori(0, (QS - 2) // 2) as r:
                n = r * 2
                loads(n, 0, 0)
                loads(n + 1, 0, 1)
            sp.wait_ge(eid_ready, NSEG)
            sp.wait_ge(scattered[1], 16 * 2 * TS)
            with sp.Fori(0, (CB - (QS - 2)) // 2) as r:
                n = r * 2 + (QS - 2)
                loads(n, 1, 0)
                loads(n + 1, 1, 1)
            results_there(0)
            for b in range(2):
                load_results(0, b, b)
            for n in range(CB, NQ - 1):
                j = group_beside(n - 1)
                store = None if j is None else lambda: store_group(j, j % 2)
                if n < NQ - 2:
                    loads(n, 1, n % 2, store)
                else:
                    load_up(n + 1, store)
                if j is not None and j + 2 < CG:
                    load_results(0, j + 2, j % 2, after=j)
            store_group(CG - 1, 1)
            results_there(1)
            for b in range(4):
                load_results(1, CG + b, b)
            with sp.Fori(0, (CG - 4) // 4) as r:
                j = r * 4 + CG
                for b in range(4):
                    store_group(j + b, b)
                    load_results(1, j + b + 4, b, after=j + b)
            for b in range(4):
                store_group(2 * CG - 4 + b, b)
            for b in range(4):
                sp.wait_ge(out_stored[b], 16 * ((CG // 2 if b < 2 else 0) + CG // 4))

        @block.tensor
        def _(pe):
            TH, TP, TH2, E, WH, HP, LO, RT = bank
            pe.wait_ge(small_in, 80)
            pe.wait_ge(const_steps, 9)
            pe.wait_ge(setup_v, 1)
            nc.tensor.transpose(TH[:, 0:P], Wg[:], ident[:])
            nc.tensor.matmul(TH[:, P:2 * P], Wg[:], a12b[:, 0, :], start=True, stop=True)
            nc.tensor.matmul(TH[:, 2 * P:3 * P], Wg[:], a12b[:, 1, :], start=True, stop=True).then_inc(setup_p, 1)
            pe.wait_ge(setup_v, 4)

            def turn(dst, src, last):
                for g in range(GG):
                    ins = nc.tensor.transpose(dst[:, g * P:(g + 1) * P], src(g), ident[:])
                ins.then_inc(last, 1)

            def iteration(i, par, has=lambda k: True):
                if has(2):
                    j = i - 2
                    if later(j, 1):
                        pe.wait_ge(probT_ready, j)
                    pe.wait_ge(exp_done, (j + 1) * GG)
                    turn(TP, lambda g: prob[:, par, g * N:(g + 1) * N], prob_turned)
                if has(4):
                    k = i - 4
                    pe.wait_ge(h2T_ready, k + 1)
                    if later(k, 1):
                        pe.wait_ge(logits_ready, k)
                    for g in range(GG):
                        ins = nc.tensor.matmul(LO[:, g * NE:(g + 1) * NE], h2T[:, g * N:(g + 1) * N], gw[:],
                                               start=True, stop=True)
                    ins.then_inc(logits_done, 1)
                if has(2):
                    pe.wait_ge(probT_ready, j + 1)
                    pe.wait_ge(wh_ready, j + 1)
                    if later(j, 1):
                        pe.wait_ge(x2_ready, j)
                    for g in range(GG):
                        ins = nc.tensor.matmul(HP[:, g * D:(g + 1) * D], probT[:, g * N:(g + 1) * N],
                                               Wh[:, par, g * D:(g + 1) * D], start=True, stop=True)
                    ins.then_inc(att_done, 1)
                if has(0):
                    pe.wait_ge(h_ready, i + 1)
                    if later(i, 1):
                        pe.wait_ge(hT_ready, i)
                    turn(TH, lambda g: h[:, par, g * D:(g + 1) * D], h_turned)
                if has(3):
                    k = i - 3
                    pe.wait_ge(h2_ready, k + 1)
                    if later(k, 1):
                        pe.wait_ge(h2T_ready, k)
                    turn(TH2, lambda g: h2[:, 1 - par, g * D:(g + 1) * D], h2_turned)
                if has(0):
                    pe.wait_ge(hT_ready, i + 1)
                    if later(i, 1):
                        pe.wait_ge(em_ready, i)
                    nc.tensor.matmul(E[:], dst_w[:], hT[:, par, :], start=True, stop=False)
                    for g in range(GG):
                        ins = nc.tensor.matmul(E[:, g * N:(g + 1) * N], hT[:, par, g * N:(g + 1) * N], src_w[:],
                                               start=False, stop=(g == GG - 1))
                    ins.then_inc(e_done, 1)
                    if later(i, 1):
                        pe.wait_ge(wh_ready, i)
                    for g in range(GG):
                        ins = nc.tensor.matmul(WH[:, g * D:(g + 1) * D], hT[:, par, g * N:(g + 1) * N], WgT[:],
                                               start=True, stop=True)
                    ins.then_inc(wh_done, 1)

            def route(s):
                pe.wait_ge(r_chosen, s + 1)
                tab = chosen[:].rearrange("p (t e) -> p t e", e=NE)
                for e in range(NE):
                    ins = nc.tensor.matmul(LO[0:TS, 64 + e:65 + e], tab[:, :, e], ones_bf[:, 0:1], start=True, stop=True)
                ins.then_inc(r_counted, 1)
                pe.wait_ge(r_cnt, 2 * s + 1)
                nc.tensor.matmul(LO[:, 128:128 + NE], ones_bf[0:TS, :], cnt[:], start=True, stop=True).then_inc(r_total, 1)
                pe.wait_ge(r_cnt, 2 * s + 2)
                nc.tensor.matmul(RT[:, 0:TE], before_bf[:], chosen[:], start=True, stop=False)
                nc.tensor.matmul(RT[:, 0:TE], ones_bf[0:TS, :], cnt_b[:], start=False, stop=True).then_inc(r_pos, 1)
                pe.wait_ge(r_read, s + 1)

            phases(pe, iteration, route)

            XP, H, O = bank[0], bank[1:5], bank[5:7]
            pe.wait_ge(weights_in, 48 * NE)
            pe.wait_ge(eid_ready, NSEG)
            pe.wait_ge(rows_ready, 2 * NSEG)

            def turn_rows(q, par):
                pe.wait_ge(xs_in, 16 * (q + 1))
                if later(q, 1):
                    pe.wait_ge(xT_ready, q)
                turn(XP, lambda k: xs_t[:, par, k, 0:D], xs_turned)

            def up(q, par, k):
                pe.wait_ge(w_in[k], 16 * (q + 1))
                if k == 0:
                    pe.wait_ge(xT_ready, q + 1)
                if later(q, 1):
                    pe.wait_ge(hid_ready, q * QT + k - (QT - 1))
                for m in range(2 * HC):
                    ins = nc.tensor.matmul(H[k][:, m * P:(m + 1) * P], w_t[:, k, m * P:(m + 1) * P],
                                           xT[:, par, k * P:(k + 1) * P], start=True, stop=True)
                ins.then_inc(up_done, 1)

            def down(q, par, k, e):
                pe.wait_ge(hid_ready, q * QT + k + 1)
                if k == 0 and later(q, 2):
                    pe.wait_ge(yo_ready, q - 1)
                for c in range(HC):
                    ins = nc.tensor.matmul(O[par][:, k * D:(k + 1) * D], hidT[:, k, c * P:(c + 1) * P],
                                           W3[:, bass.ds(e * (HC * D) + c * D, D)], start=(c == 0), stop=(c == HC - 1))
                ins.then_inc(down_done, 1)

            def quad(q, par, e_last, e, last=False):
                for k in range(QT):
                    up(q, par, k)
                    if k == 1 and not last:
                        turn_rows(q + 1, 1 - par)
                    if k >= 2:
                        down(q, par, k - 2, e[k - 2])
                    elif e_last is not None:
                        down(q - 1, 1 - par, k + 2, e_last[k + 2])

            def load_experts(q):
                return experts(mybir.EngineType.PE, q)

            turn_rows(0, 0)
            e = [load_experts(q) for q in range(3)]
            quad(0, 0, None, e[0])
            quad(1, 1, e[0], e[1])
            quad(2, 0, e[1], e[2])
            with pe.Fori(0, (NQ - 1 - 3) // 2) as r:
                q = r * 2 + 3
                e = [load_experts(q - 1), load_experts(q)]
                quad(q, 1, e[0], e[1])
                quad(q + 1, 0, e[1], load_experts(q + 1))
            e = [load_experts(NQ - 2), load_experts(NQ - 1)]
            quad(NQ - 1, 1, e[0], e[1], last=True)
            for k in (2, 3):
                down(NQ - 1, 1, k, e[1][k])

        @block.scalar
        def _(act):
            TH, TP, TH2, E, WH, HP, LO, RT = bank

            def iteration(i, par, has=lambda k: True):
                if has(2):
                    j = i - 2
                    act.wait_ge(prob_turned, j + 1)
                    if later(j, 1):
                        act.wait_ge(att_done, j)
                    nc.scalar.activation(probT[:], TP[:], ACT.Copy).then_inc(probT_ready, 1)
                if has(3):
                    k = i - 3
                    act.wait_ge(shift_ready, k + 1)
                    if later(k, 2):
                        act.wait_ge(h2_turned, k - 1)
                        act.wait_ge(h2_kept[1 - par], k // 2 * 16 if isinstance(k, int) else (k - (1 - par)) * 8)
                    for g in range(GG):
                        ins = nc.scalar.activation(h2[:, 1 - par, g * D:(g + 1) * D],
                                                   X[:, bass.ds(k * GG + g, 1), :].rearrange("p a d -> p (a d)"), ACT.Identity,
                                                   bias=shift[:, 1 - par, g:g + 1],
                                                   scale=rstd[:, 1 - par, GG + g:GG + g + 1])
                    ins.then_inc(h2_ready, 1)
                if has(0):
                    act.wait_ge(h_turned, i + 1)
                    if later(i, 2):
                        act.wait_ge(wh_done, i - 1)
                    nc.scalar.activation(hT[:, par, :], TH[:], ACT.Copy).then_inc(hT_ready, 1)
                    act.wait_ge(loaded[par], 32 * (i // 2) + 32 if isinstance(i, int) else (i - par) * 16 + 32)
                    if later(i, 2):
                        act.wait_ge(em_ready, i - 1)
                    nc.scalar.activation(mask[:, par, :], adj_t[:, par, :], ACT.Relu, scale=2 * MASKED).then_inc(mask_ready, 1)
                if has(3):
                    act.wait_ge(h2_turned, k + 1)
                    if later(k, 1):
                        act.wait_ge(logits_done, k)
                    nc.scalar.activation(h2T[:], TH2[:], ACT.Copy).then_inc(h2T_ready, 1)
                if has(1):
                    j = i - 1
                    act.wait_ge(max_ready, j + 1)
                    if later(j, 2):
                        act.wait_ge(prob_turned, j - 1)
                        act.wait_ge(inv_ready, j - 1)
                    for g in range(GG):
                        nc.scalar.activation(prob[:, 1 - par, g * N:(g + 1) * N], lr[:, 1 - par, g * N:(g + 1) * N], ACT.Exp,
                                             bias=neg_max[:, 1 - par, g:g + 1],
                                             accum_out=row_sum[:, 1 - par, g:g + 1]).then_inc(exp_done, 1)
                if has(0):
                    act.wait_ge(wh_done, i + 1)
                    if later(i, 2):
                        act.wait_ge(att_done, i - 1)
                    nc.scalar.activation(Wh[:, par, :], WH[:], ACT.Copy).then_inc(wh_ready, 1)

            def route(s):
                act.wait_ge(r_diff, s + 1)
                nc.scalar.activation(r_e[:, 1, :], r_e[:, 0, :], ACT.Exp).then_inc(r_exp, 1)

            phases(act, iteration, route)

            XP, H, O = bank[0], bank[1:5], bank[5:7]

            def copy_rows(q, par):
                act.wait_ge(xs_turned, q + 1)
                if later(q, 2):
                    act.wait_ge(up_done, (q - 1) * QT)
                nc.scalar.activation(xT[:, par, :], XP[:], ACT.Copy).then_inc(xT_ready, 1)

            def silu(t, k):
                act.wait_ge(up_done, t + 1)
                if later(t, 2):
                    act.wait_ge(hid_ready, t - 1)
                nc.scalar.activation(sil[:, k % 2, :], H[k][:, 0:HC * P], ACT.Silu).then_inc(silu_ready, 1)

            def copy_out(q, slot):
                act.wait_ge(down_done, (q + 1) * QT)
                if later(q, YB):
                    act.wait_ge(y_sent[slot], (q - slot) * (16 * QT) // YB)
                nc.scalar.activation(yo[:, slot, :], O[slot % 2][:], ACT.Copy).then_inc(yo_ready, 1)

            def quad(q, par, slot_last):
                for k in range(QT):
                    silu(q * QT + k, k)
                    if k == 1 and later(NQ - 2, q if isinstance(q, int) else 0):
                        copy_rows(q + 1, 1 - par)
                    if k == 2 and slot_last is not None:
                        copy_out(q - 1, slot_last)

            copy_rows(0, 0)
            for q in range(YB + 1):
                quad(q, q % 2, (q - 1) % YB if q > 0 else None)
            rounds = (NQ - 1 - (YB + 1)) // YB
            with act.Fori(0, rounds) as r:
                q = r * YB + (YB + 1)
                for k in range(YB):
                    quad(q + k, (k + 1) % 2, k)
            for q in range(YB + 1 + rounds * YB, NQ):
                quad(q, q % 2, (q - 1) % YB)
            copy_out(NQ - 1, (NQ - 1) % YB)

        @block.vector
        def _(dve):
            TH, TP, TH2, E, WH, HP, LO, RT = bank
            V = nc.vector

            def carry():
                dve.wait_ge(const_steps, 10)

            def row(t, i, g):
                return t[:, bass.ds(i * GG + g, 1), :].rearrange("p a d -> p (a d)")

            def stats_of(i, batch_par, col, bn):
                for g in range(GG):
                    ins = V.bn_stats(stats[:, batch_par, col + g, :], row(X, i, g))
                ins.then_inc(bn, 1)

            def aggregate(batch_par, col, ag):
                for g in range(GG):
                    V.bn_aggr(mv[:, batch_par, col + g, :], stats[:, batch_par, col + g, :]).then_inc(ag, 1)

            def normalize(i, dst, col, batch_par):
                for g in range(GG):
                    ins = V.tensor_scalar(dst(g), row(X, i, g), mv[:, batch_par, col + g, 0:1],
                                          rstd[:, batch_par, col + g:col + g + 1], ALU.subtract, ALU.mult)
                return ins

            def add_eps(i, batch_par, col, ag, var):
                dve.wait_ge(ag, (i + 1) * GG)
                V.tensor_scalar(var_eps[:, batch_par, col:col + GG], mv[:, batch_par, col:col + GG, 1], EPS, None, ALU.add)\
                    .then_inc(var, 1)

            def first_stats(i, par):
                dve.wait_ge(loaded[par], 32 * (i // 2) + 32 if isinstance(i, int) else (i - par) * 16 + 32)
                return i

            def iteration(i, par, has=lambda k: True):
                if has(1):
                    dve.wait_ge(e_done, i)
                    dve.wait_ge(mask_ready, i)
                    if later(i, 2):
                        dve.wait_ge(lr_ready, i - 1)
                    V.scalar_tensor_tensor(em[:], mask[:, 1 - par, :], -MASKED, E[:], ALU.add, ALU.min).then_inc(em_ready, 1)
                if has(0):
                    dve.wait_ge(rstd1_ready, i + 1)
                    if later(i, 2):
                        dve.wait_ge(h_turned, i - 1)
                    normalize(i, lambda g: h[:, par, g * D:(g + 1) * D], 0, 1 - par).then_inc(h_ready, 1)
                if has(1):
                    dve.wait_ge(em_ready, i)
                    if later(i, 3):
                        dve.wait_ge(exp_done, (i - 2) * GG)
                    V.scalar_tensor_tensor(lr[:, 1 - par, :], em[:], SLOPE, em[:], ALU.mult, ALU.max).then_inc(lr_ready, 1)
                if has(3):
                    dve.wait_ge(rstd2_ready, i - 2)
                    V.scalar_tensor_tensor(shift[:, 1 - par, :], mv[:, 1 - par, GG:2 * GG, 0], -1.0,
                                           rstd[:, 1 - par, GG:2 * GG], ALU.mult, ALU.mult).then_inc(shift_ready, 1)
                if has(2):
                    j = i - 2
                    dve.wait_ge(exp_done, (j + 1) * GG)
                    V.reciprocal(row_inv[:], row_sum[:, par, :]).then_inc(inv_ready, 1)
                if has(-1):
                    carry()
                    first_stats(i + 1, 1 - par)
                    stats_of(i + 1, par, 0, bn1)
                if has(1):
                    dve.wait_ge(lr_ready, i)
                    V.tensor_reduce(neg_max[:, 1 - par, :], lr[:, 1 - par, :].rearrange("p (g m) -> p g m", m=N), AX.X, ALU.max,
                                    negate=True).then_inc(max_ready, 1)
                if has(-1):
                    dve.wait_ge(bn1, i + 2)
                if has(2):
                    dve.wait_ge(inv_ready, j + 1)
                    dve.wait_ge(att_done, j + 1)
                    for g in range(GG):
                        ins = V.scalar_tensor_tensor(row(X, j, g), HP[:, g * D:(g + 1) * D], row_inv[:, g:g + 1],
                                                     row(X, j, g), ALU.mult, ALU.add)
                    ins.then_inc(x2_ready, 1)
                if has(-1):
                    aggregate(par, 0, ag1)
                if has(2):
                    carry()
                    dve.wait_ge(x2_ready, j + 1)
                    stats_of(j, par, GG, bn2)
                if has(-1):
                    add_eps(i + 1, par, 0, ag1, var1_ready)
                if has(2):
                    dve.wait_ge(bn2, j + 1)
                if has(4):
                    k = i - 4
                    dve.wait_ge(logits_done, k + 1)
                    V.tensor_tensor(LG[:, bass.ds(k * GG, GG), :], LO[:, 0:GG * NE].rearrange("p (g e) -> p g e", e=NE),
                                    gb[:].rearrange("p (o e) -> p o e", o=1).broadcast_to([P, GG, NE]), ALU.add)\
                        .then_inc(logits_ready, 1)
                if has(2):
                    aggregate(par, GG, ag2)
                    add_eps(j, par, GG, ag2, var2_ready)

            steps = [0]

            def link(ins):
                steps[0] += 1
                ins.then_inc(r_steps, 1)
                dve.wait_ge(r_steps, steps[0])

            def te(ap):
                return ap.rearrange("p (t e) -> p t e", e=NE)

            def route(s):
                def per_tile(ap):
                    return ap.rearrange("p (t o) -> p t o", o=1).broadcast_to([P, TS, NE])

                def per_expert(ap, n):
                    return ap.rearrange("p (o e) -> p o e", o=1).broadcast_to([P, n, NE])

                dve.wait_ge(logits_ready, (s + 1) * IS)
                logits = LG[:, s * TS:(s + 1) * TS, :]
                for c in range(2):
                    L = logits if c == 0 else te(r_l2[:])
                    link(V.tensor_reduce(r_m[:, c, :], L, AX.X, ALU.max))
                    link(V.tensor_tensor(te(r_a[:]), L, per_tile(r_m[:, c, :]), ALU.is_equal))
                    link(V.tensor_tensor(te(r_b[:]), te(r_a[:]), per_expert(e_rank[:], TS), ALU.mult))
                    link(V.tensor_reduce(r_m[:, 2 + c, :], te(r_b[:]), AX.X, ALU.max))
                    link(V.tensor_tensor(te(oh[:, c, :]), te(r_b[:]), per_tile(r_m[:, 2 + c, :]), ALU.is_equal))
                    if c == 0:
                        link(V.scalar_tensor_tensor(r_l2[:], oh[:, 0, :], -3e38,
                                                    logits.rearrange("p t e -> p (t e)"), ALU.mult, ALU.add))
                V.tensor_tensor(chosen[:], oh[:, 0, :], oh[:, 1, :], ALU.add).then_inc(r_chosen, 1)
                V.tensor_tensor(r_e[:, 0, :], r_m[:, 1, :], r_m[:, 0, :], ALU.subtract).then_inc(r_diff, 1)
                dve.wait_ge(r_counted, s + 1)
                V.tensor_copy(cnt[:], LO[0:TS, 64:64 + NE]).then_inc(r_cnt, 1)
                dve.wait_ge(r_cnt, 2 * s + 1)
                V.tensor_tensor(te(cnt_b[:]),
                                before[0:TS, 0:TS].rearrange("p (t o) -> p t o", o=1).broadcast_to([TS, TS, NE]),
                                cnt[:].rearrange("p (o e) -> p o e", o=1).broadcast_to([TS, TS, NE]), ALU.mult).then_inc(r_cnt, 1)
                dve.wait_ge(r_total, s + 1)
                V.tensor_scalar(r_c[:], LO[:, 128:128 + NE], 1.0 / P, 0.498, ALU.mult, ALU.add).then_inc(r_read, 1)
                dve.wait_ge(r_read, s + 1)
                link(V.tensor_scalar(r_cr[:], r_c[:], float(2 ** 23), None, ALU.add))
                link(V.tensor_scalar(r_t[:, 0, :], r_cr[:], float(2 ** 23), None, ALU.subtract))
                link(V.tensor_tensor(r_ee[:], e_before[:], per_expert(r_t[:, 0, :], NE), ALU.mult))
                link(V.tensor_reduce(r_t[:, 1, :], r_ee[:], AX.X, ALU.add))
                link(V.tensor_scalar(r_t[:, 3, :], r_t[:, 1, :], float(P), None, ALU.mult))
                dve.wait_ge(r_pos, s + 1)
                link(V.tensor_tensor(te(r_a[:]), te(RT[:, 0:TE]), per_expert(r_t[:, 3, :], TS), ALU.add))
                for c in range(2):
                    link(V.tensor_tensor(r_b[:], oh[:, c, :], r_a[:], ALU.mult))
                    link(V.tensor_reduce(r_row[:, c, :], te(r_b[:]), AX.X, ALU.add))
                    V.tensor_copy(ROW[:, s, c, :], r_row[:, c, :]).then_inc(rows_ready, 1)
                gates = GATE[:, :, s * TS:(s + 1) * TS]
                dve.wait_ge(r_exp, s + 1)
                link(V.tensor_scalar(r_e[:, 2, :], r_e[:, 1, :], 1.0, None, ALU.add))
                link(V.reciprocal(gates[:, 0, :], r_e[:, 2, :]))
                link(V.tensor_tensor(gates[:, 1, :], r_e[:, 1, :], gates[:, 0, :], ALU.mult))
                link(V.tensor_tensor(r_t[:, 2, :], r_t[:, 1, :], r_t[:, 0, :], ALU.add))
                dve.wait_ge(rows_ready, 2 * s + 2)
                link(V.tensor_tensor(r_id[:], r_t[0:1, 2, 0:NE - 1].rearrange("p (o e) -> p o e", o=1).broadcast_to([1, NT, NE - 1]),
                                     tile_no[:].rearrange("p (j o) -> p j o", o=1).broadcast_to([1, NT, NE - 1]), ALU.is_le))
                link(V.tensor_reduce(r_idf[:], r_id[:], AX.X, ALU.add))
                V.tensor_copy(EID[0:1, s * NT:(s + 1) * NT], r_idf[:]).then_inc(eid_ready, 1)

            first_stats(0, 0)
            stats_of(0, 1, 0, bn1)
            dve.wait_ge(bn1, 1)
            aggregate(1, 0, ag1)
            add_eps(0, 1, 0, ag1, var1_ready)
            dve.wait_ge(small_in, 80)
            for k in range(2):
                ins = V.tensor_copy(a12b[:, k, :], a12[:, k:k + 1].broadcast_to([P, P]))
            ins.then_inc(setup_v, 1)
            dve.wait_ge(setup_p, 1)
            V.tensor_copy(WgT[:], TH[:, 0:P]).then_inc(setup_v, 1)
            V.tensor_copy(src_w[:], TH[:, P:2 * P]).then_inc(setup_v, 1)
            V.tensor_copy(dst_w[:], TH[:, 2 * P:3 * P]).then_inc(setup_v, 1)
            dve.wait_ge(const_steps, 10)
            phases(dve, iteration, route)

            H = bank[1:5]

            def gate_hidden(t, k):
                dve.wait_ge(silu_ready, t + 1)
                if later(t, QT):
                    dve.wait_ge(down_done, t - (QT - 1))
                V.tensor_tensor(hidT[:, k, :], sil[:, k % 2, :], H[k][:, HC * P:2 * HC * P], ALU.mult).then_inc(hid_ready, 1)

            def keep_dest(q, par):
                dve.wait_ge(xs_in, 16 * (q + 1))
                dest = DEST[:, bass.ds(q * QT, QT)]
                V.tensor_tensor(dest, dest, xs_t[:, par, :, D].bitcast(U32), ALU.max)\
                    .then_inc(dest_ready, 1)

            def quad(q, par_next=None, middle=None):
                for k in range(QT):
                    gate_hidden(q * QT + k, k)
                    if k == 1 and middle is not None:
                        middle()
                    if k == 1 and par_next is not None:
                        keep_dest(q + 1, par_next)

            def add_first(j, b, there):
                dve.wait_ge(y_in[b], there)
                for k in range(QT):
                    ins = V.scalar_tensor_tensor(part[b][:, k, :], got[b][:, k, 0, :], GATE[:, 0, bass.ds(j * QT + k, 1)],
                                                 row(X, j, k), ALU.mult, ALU.add)
                ins.then_inc(part_ready, 1)

            def add_second(j, b, stored):
                dve.wait_ge(part_ready, j + 1)
                if stored is not None:
                    dve.wait_ge(out_stored[b], stored)
                for k in range(QT):
                    ins = V.scalar_tensor_tensor(res[b][:, k, :], got[b][:, k, 1, :], GATE[:, 1, bass.ds(j * QT + k, 1)],
                                                 part[b][:, k, :], ALU.mult, ALU.add)
                ins.then_inc(res_ready, 1)

            def combine(j, b, there, stored):
                add_first(j, b, there)
                add_second(j, b, stored)

            keep_dest(0, 0)
            quad(0, 1)
            quad(1, 0)
            with dve.Fori(0, (CB - 2) // 2) as r:
                q = r * 2 + 2
                quad(q, 1)
                quad(q + 1, 0)
            for q in range(CB, NQ):
                j_last, j = group_beside(q - 1), group_beside(q)
                quad(q, 1 - q % 2 if q < NQ - 1 else None,
                     None if j_last is None else lambda: add_second(j_last, j_last % 2, 16 * (j_last // 2) if j_last >= 2 else None))
                if j is not None:
                    add_first(j, j % 2, 16 * (j // 2 + 1))
            seg0 = [16 * CG // 2 if b < 2 else 0 for b in range(4)]
            for b in range(4):
                combine(CG + b, b, seg0[b] + 16, seg0[b] or None)
            with dve.Fori(0, (CG - 4) // 4) as r:
                for b in range(4):
                    combine(r * 4 + (CG + 4 + b), b, r * 16 + (seg0[b] + 32), r * 16 + (seg0[b] + 16))

        @block.gpsimd
        def _(pool):
            g = nc.gpsimd
            g.memset(zeros[:], 0.0).then_inc(consts, 1)
            g.iota(H2[:, :, D].bitcast(I32), pattern=[[0, NSEG], [2 * P, TS]], base=NT * P, channel_multiplier=2).then_inc(dest_steps, 1)
            g.memset(half_neg[:], -0.5).then_inc(const_steps, 1)
            g.memset(ident[:], 0.0).then_inc(const_steps, 1)
            g.memset(before[:], 1.0).then_inc(const_steps, 1)
            g.memset(ones_bf[:], 1.0).then_inc(const_steps, 1)
            g.memset(e_before[:], 1.0).then_inc(const_steps, 1)
            pool.wait_ge(const_steps, 5)
            g.affine_select(out=ident[:], in_=ident[:], compare_op=ALU.not_equal, fill=1.0, base=0,
                            pattern=[[-1, P]], channel_multiplier=1).then_inc(const_steps, 1)
            g.affine_select(out=before[:], in_=before[:], compare_op=ALU.is_gt, fill=0.0, base=0,
                            pattern=[[1, P]], channel_multiplier=-1).then_inc(const_steps, 1)
            g.affine_select(out=e_before[:], in_=e_before[:], compare_op=ALU.is_gt, fill=0.0, base=0,
                            pattern=[[1, NE], [-1, NE]], channel_multiplier=0).then_inc(const_steps, 1)
            pool.wait_ge(const_steps, 8)
            g.tensor_copy(before_bf[:], before[:]).then_inc(const_steps, 1)
            g.iota(DEST[:].bitcast(I32), pattern=[[0, NSEG], [P, NT]], base=0, channel_multiplier=1)
            g.iota(e_rank[:], pattern=[[-1, NE]], base=NE, channel_multiplier=0, allow_small_or_imprecise_dtypes=True)
            g.iota(tile_no[:], pattern=[[1, NT]], base=0, channel_multiplier=0, allow_small_or_imprecise_dtypes=True).then_inc(const_steps, 1)

            def root(var, rstd_done, i, par, col, read):
                pool.wait_ge(var, i + 1)
                if i >= 2:
                    pool.wait_ge(read, i - 1)
                g.tensor_tensor(rstd[:, par, col:col + GG], var_eps[:, par, col:col + GG], half_neg[:], ALU.pow).then_inc(rstd_done, 1)

            def scatter(s, n):
                c, t = n // TS, n % TS
                if t == 0:
                    pool.wait_ge(rows_ready, 2 * s + c + 1)
                if n == TS:
                    pool.wait_ge(scattered[s], 16 * TS)
                    g.iota(H2[:, s * TS:(s + 1) * TS, D].bitcast(I32), pattern=[[2 * P, TS]], base=NT * P + 1,
                           channel_multiplier=2).then_inc(dest_steps, 1)
                    pool.wait_ge(dest_steps, 2 + s)
                pool.indirect_dma_start(xs[s], bass.IndirectOffsetOnAxis(ap=ROW[:, s, c, t:t + 1], axis=0),
                                        H2[:, s * TS + t, :], None).then_inc(scattered[s], 16)

            def send(q):
                pool.wait_ge(dest_ready, q + 1)
                pool.wait_ge(yo_ready, q + 1)
                for k in range(QT):
                    pool.indirect_dma_start(ys[q // QS], bass.IndirectOffsetOnAxis(ap=DEST[:, q * QT + k:q * QT + k + 1], axis=0),
                                            yo[:, q % YB, k * D:(k + 1) * D], None).then_inc(y_sent[q % YB], 16)

            n = 0
            for i in range(-1, NI + 2):
                if i == IS + 4:
                    pool.wait_ge(zeroed[0], 16 * IS)
                    for par in range(2):
                        pool.wait_ge(h2_kept[par], 8 * IS)
                if i >= IS + 4:
                    for _ in range(6):
                        scatter(0, n)
                        n += 1
                if i + 1 < NI:
                    root(var1_ready, rstd1_ready, i + 1, i % 2, 0, h_ready)
                if i >= 2:
                    root(var2_ready, rstd2_ready, i - 2, i % 2, GG, h2_ready)
            for m in range(n, 2 * TS):
                scatter(0, m)
            pool.wait_ge(zeroed[1], 16 * IS)
            for par in range(2):
                pool.wait_ge(h2_kept[par], 8 * NI)
            AHEAD, EACH = 26, 5
            n = 0
            for q in range(NQ):
                for _ in range(AHEAD if q == 0 else EACH):
                    if n < 2 * TS:
                        scatter(1, n)
                        n += 1
                send(q)


_INS = ['x', 'adj', 'L0_gnn_W', 'L0_gnn_a', 'L0_ffn_gate_w', 'L0_ffn_gate_b', 'L0_ffn_w1', 'L0_ffn_w2', 'L0_ffn_w3']
_OUTS = [((64, 128, 128), 'float32')]


def kernel(**inputs):
    import numpy as _np
    import concourse.bacc as _bacc
    from concourse import mybir as _mybir
    from concourse.bass_utils import run_bass_kernel_spmd as _run

    nc = _bacc.Bacc("TRN2", target_bir_lowering=False, num_devices=1)
    arrays, args = {}, []
    for name in _INS:
        a = _np.ascontiguousarray(inputs[name])
        arrays[f"in_{name}_dram"] = a
        args.append(nc.dram_tensor(f"in_{name}_dram", a.shape, _mybir.dt.from_np(a.dtype), kind="ExternalInput").ap())
    for i, (shape, dtype) in enumerate(_OUTS):
        dt = _mybir.dt.from_np(_np.dtype(dtype))
        args.append(nc.dram_tensor(f"out_{i}_dram", shape, dt, kind="ExternalOutput").ap())
    gat_moe_kernel(nc, *args)
    r = _run(nc, [arrays], core_ids=[0])
    return r.results[0]["out_0_dram"]
```
